# Optimizing a Trainium2 kernel written in Bass

```python
import numpy as np
import jax
import jax.numpy as jnp

def _softmax(x, axis=-1):
    return jax.nn.softmax(x, axis=axis)

def _gelu(x):
    return jax.nn.gelu(x, approximate=True)

def _silu(x):
    return jax.nn.silu(x)

def _sigmoid(x):
    return jax.nn.sigmoid(x)

def _layernorm(x, axis=-1, eps=1e-05):
    m = jnp.mean(x, axis=axis, keepdims=True)
    v = jnp.var(x, axis=axis, keepdims=True)
    return (x - m) / jnp.sqrt(v + eps)

def _scatter_add(tgt, idx, src, axis=0):
    return tgt.at[idx].add(src)

def _segment_sum(src, seg, n):
    return jax.ops.segment_sum(src, seg, n)
kernel_name = 'mk_flamingo_gated_d2_seqx_r4_22219c'

def setup_inputs(seed: int=0):
    np.random.seed(seed)
    _w = jnp.asarray

    def _rec_inputs():
        import jax
        import jax.numpy as jnp
        _rk = jax.random.key(seed)
        x = -0.0002928 + 1 * jax.random.normal(jax.random.fold_in(_rk, 1), (1, 2048, 256), jnp.float32)
        _lenS = 2048 - jax.random.randint(jax.random.fold_in(_rk, 7), (1,), 0, max(1, 2048 // 4) + 1, jnp.int32)
        _lenS2 = 1601 - jax.random.randint(jax.random.fold_in(_rk, 8), (1,), 0, max(1, 1601 // 4) + 1, jnp.int32)
        _ctx_1024P = jax.random.normal(jax.random.fold_in(_rk, 11), (1, 16, 256), jnp.float32)
        _ctx_1024c = jax.random.dirichlet(jax.random.fold_in(_rk, 511), 0.3 * jnp.ones((16,), jnp.float32), (1, 1601))
        _ctx_1024t = jnp.einsum('bsk,bkd->bsd', _ctx_1024c, _ctx_1024P)
        _ctx_1024t = _ctx_1024t * jax.lax.rsqrt(jnp.mean(jnp.square(_ctx_1024t)) + 1e-12) * 0.953939
        ctx_1024 = -1.39393e-06 + 0.999914 * (_ctx_1024t + 0.3 * jax.random.normal(jax.random.fold_in(_rk, 611), (1, 1601, 256), jnp.float32))
        _validS = jnp.arange(2048)[None, :] < _lenS[:, None]
        _validS2 = jnp.arange(1601)[None, :] < _lenS2[:, None]
        _causal = jnp.tril(jnp.ones((2048, 2048), dtype=bool))
        mask_Bx1xSxS2_bf0 = jnp.logical_not(jnp.ones((1, 1, 2048, 1601), dtype=bool))
        _g = jax.random.normal(jax.random.fold_in(_rk, 9001), (2, 2), jnp.float32)
        _g = jnp.sign(_g) * jnp.maximum(jnp.abs(_g), 1.0) + (_g == 0) * 1.0
        g_xattn = _g[0]
        g_ffn = _g[1]
        return (x, ctx_1024, mask_Bx1xSxS2_bf0, g_xattn, g_ffn)
    x, ctx_1024, mask_Bx1xSxS2_bf0, g_xattn, g_ffn = _rec_inputs()

    def _L0_xattn_setup():
        import jax, jax.numpy as jnp
        import numpy as np
        B, S, D, H = (2, 512, 256, 16)
        HD = D // H
        LN_EPS = 1e-05

        def _linear(x, w, b):
            return jnp.einsum('bsd,od->bso', x, w) + b

        def _split_heads(x):
            b, s, _ = x.shape
            return x.reshape(b, s, H, HD).transpose(0, 2, 1, 3)
        key = jax.random.key(seed)
        ks = jax.random.split(key, 14)
        w = 0.02
        return {'q': jax.random.normal(ks[0], (B, S, D), jnp.float32), 'k': jax.random.normal(ks[1], (B, S, D), jnp.float32), 'v': jax.random.normal(ks[2], (B, S, D), jnp.float32), 'mask': jnp.zeros((B, 1, S, S), dtype=bool), 'training': 0, 'wq_w': jax.random.normal(ks[3], (D, D), jnp.float32) * w, 'wq_b': jnp.zeros((D,), jnp.float32), 'wk_w': jax.random.normal(ks[4], (D, D), jnp.float32) * w, 'wk_b': jnp.zeros((D,), jnp.float32), 'wv_w': jax.random.normal(ks[5], (D, D), jnp.float32) * w, 'wv_b': jnp.zeros((D,), jnp.float32), 'wo_w': jax.random.normal(ks[6], (D, D), jnp.float32) * w, 'wo_b': jnp.zeros((D,), jnp.float32), 'ln_g': jnp.ones((D,), jnp.float32), 'ln_b': jnp.zeros((D,), jnp.float32)}
    _L0_xattn_all = _L0_xattn_setup()
    _L0_xattn_in = {k: v for k, v in _L0_xattn_all.items() if k in ('wq_w', 'wq_b', 'wk_w', 'wk_b', 'wv_w', 'wv_b', 'wo_w', 'wo_b', 'ln_g', 'ln_b')}
    del _L0_xattn_all

    def _L0_ffn_setup():
        import jax, jax.numpy as jnp
        import numpy as np
        DIM = 256
        HIDDEN = 768
        SCALE = 1.0 / 127.0

        def _dequant(w_int, dtype):
            return w_int.astype(dtype) * jnp.asarray(SCALE, dtype)
        key = jax.random.key(seed)
        k_x, k_g, k_u, k_d = jax.random.split(key, 4)
        x = jax.random.normal(k_x, (4, 512, DIM), dtype=jnp.float32)
        w_gate = jax.random.randint(k_g, (HIDDEN, DIM), -127, 128, dtype=jnp.int32)
        w_up = jax.random.randint(k_u, (HIDDEN, DIM), -127, 128, dtype=jnp.int32)
        w_down = jax.random.randint(k_d, (DIM, HIDDEN), -127, 128, dtype=jnp.int32)
        return {'x': x, 'w_gate': w_gate, 'w_up': w_up, 'w_down': w_down}
    _L0_ffn_all = _L0_ffn_setup()
    _L0_ffn_in = {k: v for k, v in _L0_ffn_all.items() if k in ('w_gate', 'w_up', 'w_down')}
    del _L0_ffn_all

    def _L1_xattn_setup():
        import jax, jax.numpy as jnp
        import numpy as np
        D_MODEL = 256
        NUM_HEADS = 16
        HEAD_DIM = D_MODEL // NUM_HEADS
        key = jax.random.key(seed)
        ks = jax.random.split(key, 11)
        B, S = (2, 512)
        s = 1.0 / np.sqrt(D_MODEL)
        inp = {'query': jax.random.normal(ks[0], (B, S, D_MODEL), jnp.float32), 'key': jax.random.normal(ks[1], (B, S, D_MODEL), jnp.float32), 'value': jax.random.normal(ks[2], (B, S, D_MODEL), jnp.float32), 'Wq': jax.random.normal(ks[3], (D_MODEL, D_MODEL), jnp.float32) * s, 'bq': jax.random.normal(ks[4], (D_MODEL,), jnp.float32) * s, 'Wk': jax.random.normal(ks[5], (D_MODEL, D_MODEL), jnp.float32) * s, 'bk': jax.random.normal(ks[6], (D_MODEL,), jnp.float32) * s, 'Wv': jax.random.normal(ks[7], (D_MODEL, D_MODEL), jnp.float32) * s, 'bv': jax.random.normal(ks[8], (D_MODEL,), jnp.float32) * s, 'Wo': jax.random.normal(ks[9], (D_MODEL, D_MODEL), jnp.float32) * s, 'bo': jax.random.normal(ks[10], (D_MODEL,), jnp.float32) * s}
        return inp
    _L1_xattn_all = _L1_xattn_setup()
    _L1_xattn_in = {k: v for k, v in _L1_xattn_all.items() if k in ('Wq', 'bq', 'Wk', 'bk', 'Wv', 'bv', 'Wo', 'bo')}
    del _L1_xattn_all

    def _L1_ffn_setup():
        import jax, jax.numpy as jnp
        import numpy as np
        H = 256
        I = 176
        E = 64
        TOP_K = 8
        NG = 8
        TOPK_GROUP = 4
        N_SHARED = 2
        ROUTED_SCALE = 2.5
        S_I = I * N_SHARED

        def _route(x, gate_w, gate_bias):
            T = x.shape[0]
            logits = x @ gate_w.T
            scores = jax.nn.sigmoid(logits)
            scores_for_choice = scores + gate_bias[None, :]
            grp = scores_for_choice.reshape(T, NG, E // NG)
            group_scores = jnp.sum(jax.lax.top_k(grp, 2)[0], axis=-1)
            _, gidx = jax.lax.top_k(group_scores, TOPK_GROUP)
            gmask = jnp.zeros((T, NG), dtype=scores.dtype).at[jnp.arange(T)[:, None], gidx].set(1.0)
            emask = jnp.repeat(gmask, E // NG, axis=1)
            masked = jnp.where(emask > 0, scores_for_choice, 0.0)
            _, topk_idx = jax.lax.top_k(masked, TOP_K)
            topk_w = jnp.take_along_axis(scores, topk_idx, axis=1)
            topk_w = topk_w / (jnp.sum(topk_w, axis=-1, keepdims=True) + 1e-20)
            topk_w = topk_w * ROUTED_SCALE
            rw = jnp.zeros((T, E), dtype=scores.dtype).at[jnp.arange(T)[:, None], topk_idx].add(topk_w)
            return rw

        def _mlp(x, gw, uw, dw):
            return jax.nn.silu(x @ gw.T) * (x @ uw.T) @ dw.T
        key = jax.random.key(seed)
        ks = jax.random.split(key, 10)
        sc = 0.02
        return {'hidden_states': jax.random.normal(ks[0], (1, 256, H), dtype=jnp.float32), 'gate_w': sc * jax.random.normal(ks[1], (E, H), dtype=jnp.float32), 'gate_bias': sc * jax.random.normal(ks[2], (E,), dtype=jnp.float32), 'Wg': sc * jax.random.normal(ks[3], (E, I, H), dtype=jnp.float32), 'Wu': sc * jax.random.normal(ks[4], (E, I, H), dtype=jnp.float32), 'Wd': sc * jax.random.normal(ks[5], (E, H, I), dtype=jnp.float32), 'Sg': sc * jax.random.normal(ks[6], (S_I, H), dtype=jnp.float32), 'Su': sc * jax.random.normal(ks[7], (S_I, H), dtype=jnp.float32), 'Sd': sc * jax.random.normal(ks[8], (H, S_I), dtype=jnp.float32)}
    _L1_ffn_all = _L1_ffn_setup()
    _L1_ffn_in = {k: v for k, v in _L1_ffn_all.items() if k in ('gate_w', 'gate_bias', 'Wg', 'Wu', 'Wd', 'Sg', 'Su', 'Sd')}
    del _L1_ffn_all
    return {'x': x, 'ctx_1024': ctx_1024, 'mask_Bx1xSxS2_bf0': mask_Bx1xSxS2_bf0, 'g_xattn': g_xattn, 'g_ffn': g_ffn, 'L0_xattn_wq_w': _L0_xattn_in['wq_w'], 'L0_xattn_wq_b': _L0_xattn_in['wq_b'], 'L0_xattn_wk_w': _L0_xattn_in['wk_w'], 'L0_xattn_wk_b': _L0_xattn_in['wk_b'], 'L0_xattn_wv_w': _L0_xattn_in['wv_w'], 'L0_xattn_wv_b': _L0_xattn_in['wv_b'], 'L0_xattn_wo_w': _L0_xattn_in['wo_w'], 'L0_xattn_wo_b': _L0_xattn_in['wo_b'], 'L0_xattn_ln_g': _L0_xattn_in['ln_g'], 'L0_xattn_ln_b': _L0_xattn_in['ln_b'], 'L0_ffn_w_gate': _L0_ffn_in['w_gate'], 'L0_ffn_w_up': _L0_ffn_in['w_up'], 'L0_ffn_w_down': _L0_ffn_in['w_down'], 'L1_xattn_Wq': _L1_xattn_in['Wq'], 'L1_xattn_bq': _L1_xattn_in['bq'], 'L1_xattn_Wk': _L1_xattn_in['Wk'], 'L1_xattn_bk': _L1_xattn_in['bk'], 'L1_xattn_Wv': _L1_xattn_in['Wv'], 'L1_xattn_bv': _L1_xattn_in['bv'], 'L1_xattn_Wo': _L1_xattn_in['Wo'], 'L1_xattn_bo': _L1_xattn_in['bo'], 'L1_ffn_gate_w': _L1_ffn_in['gate_w'], 'L1_ffn_gate_bias': _L1_ffn_in['gate_bias'], 'L1_ffn_Wg': _L1_ffn_in['Wg'], 'L1_ffn_Wu': _L1_ffn_in['Wu'], 'L1_ffn_Wd': _L1_ffn_in['Wd'], 'L1_ffn_Sg': _L1_ffn_in['Sg'], 'L1_ffn_Su': _L1_ffn_in['Su'], 'L1_ffn_Sd': _L1_ffn_in['Sd']}

def reference(x, ctx_1024, mask_Bx1xSxS2_bf0, g_xattn, g_ffn, L0_xattn_wq_w, L0_xattn_wq_b, L0_xattn_wk_w, L0_xattn_wk_b, L0_xattn_wv_w, L0_xattn_wv_b, L0_xattn_wo_w, L0_xattn_wo_b, L0_xattn_ln_g, L0_xattn_ln_b, L0_ffn_w_gate, L0_ffn_w_up, L0_ffn_w_down, L1_xattn_Wq, L1_xattn_bq, L1_xattn_Wk, L1_xattn_bk, L1_xattn_Wv, L1_xattn_bv, L1_xattn_Wo, L1_xattn_bo, L1_ffn_gate_w, L1_ffn_gate_bias, L1_ffn_Wg, L1_ffn_Wu, L1_ffn_Wd, L1_ffn_Sg, L1_ffn_Su, L1_ffn_Sd):
    import jax
    import jax.numpy as jnp

    def _L0_xattn_ref(q, k, v, mask, training, wq_w, wq_b, wk_w, wk_b, wv_w, wv_b, wo_w, wo_b, ln_g, ln_b):
        import jax, jax.numpy as jnp
        import numpy as np
        B, S, D, H = (2, 512, 256, 16)
        HD = D // H
        LN_EPS = 1e-05

        def _linear(x, w, b):
            return jnp.einsum('bsd,od->bso', x, w) + b

        def _split_heads(x):
            b, s, _ = x.shape
            return x.reshape(b, s, H, HD).transpose(0, 2, 1, 3)
        residual = q
        Q = _split_heads(_linear(q, wq_w, wq_b))
        K = _split_heads(_linear(k, wk_w, wk_b))
        V = _split_heads(_linear(v, wv_w, wv_b))
        dk = jnp.sqrt(jnp.asarray(HD, jnp.float16)).astype(jnp.float32) + 1e-08
        score = jnp.einsum('bhqd,bhkd->bhqk', Q, K) / dk
        attn = jnp.where(mask, -jnp.inf, score)
        ctx = jnp.einsum('bhqk,bhkd->bhqd', attn, V)
        b, _, s, _ = ctx.shape
        ctx = ctx.transpose(0, 2, 1, 3).reshape(b, s, D)
        o = _linear(ctx, wo_w, wo_b)
        x = residual + o
        mu = jnp.mean(x, axis=-1, keepdims=True)
        var = jnp.mean(jnp.square(x - mu), axis=-1, keepdims=True)
        return ln_g * (x - mu) * jax.lax.rsqrt(var + LN_EPS) + ln_b

    def _L0_ffn_ref(x, w_gate, w_up, w_down):
        import jax, jax.numpy as jnp
        import numpy as np
        DIM = 256
        HIDDEN = 768
        SCALE = 1.0 / 127.0

        def _dequant(w_int, dtype):
            return w_int.astype(dtype) * jnp.asarray(SCALE, dtype)
        wg = _dequant(w_gate, x.dtype)
        wu = _dequant(w_up, x.dtype)
        wd = _dequant(w_down, x.dtype)
        gate = jnp.einsum('bsd,hd->bsh', x, wg)
        up = jnp.einsum('bsd,hd->bsh', x, wu)
        h = jax.nn.silu(gate) * up
        return jnp.einsum('bsh,dh->bsd', h, wd)

    def _L1_xattn_ref(query, key, value, Wq, bq, Wk, bk, Wv, bv, Wo, bo):
        import jax, jax.numpy as jnp
        import numpy as np
        D_MODEL = 256
        NUM_HEADS = 16
        HEAD_DIM = D_MODEL // NUM_HEADS
        B, Sq, _ = query.shape

        def proj(x, W, b):
            y = x @ W.T + b
            return y.reshape(B, -1, NUM_HEADS, HEAD_DIM).transpose(0, 2, 1, 3)
        Q = proj(query, Wq, bq)
        K = proj(key, Wk, bk)
        V = proj(value, Wv, bv)
        scale = 1.0 / jnp.sqrt(jnp.asarray(HEAD_DIM, Q.dtype))
        scores = jnp.einsum('bhqd,bhkd->bhqk', Q, K) * scale
        attn = jax.nn.softmax(scores, axis=-1)
        out = jnp.einsum('bhqk,bhkd->bhqd', attn, V)
        out = out.transpose(0, 2, 1, 3).reshape(B, Sq, NUM_HEADS * HEAD_DIM)
        return out @ Wo.T + bo

    def _L1_ffn_ref(hidden_states, gate_w, gate_bias, Wg, Wu, Wd, Sg, Su, Sd):
        import jax, jax.numpy as jnp
        import numpy as np
        H = 256
        I = 176
        E = 64
        TOP_K = 8
        NG = 8
        TOPK_GROUP = 4
        N_SHARED = 2
        ROUTED_SCALE = 2.5
        S_I = I * N_SHARED

        def _route(x, gate_w, gate_bias):
            T = x.shape[0]
            logits = x @ gate_w.T
            scores = jax.nn.sigmoid(logits)
            scores_for_choice = scores + gate_bias[None, :]
            grp = scores_for_choice.reshape(T, NG, E // NG)
            group_scores = jnp.sum(jax.lax.top_k(grp, 2)[0], axis=-1)
            _, gidx = jax.lax.top_k(group_scores, TOPK_GROUP)
            gmask = jnp.zeros((T, NG), dtype=scores.dtype).at[jnp.arange(T)[:, None], gidx].set(1.0)
            emask = jnp.repeat(gmask, E // NG, axis=1)
            masked = jnp.where(emask > 0, scores_for_choice, 0.0)
            _, topk_idx = jax.lax.top_k(masked, TOP_K)
            topk_w = jnp.take_along_axis(scores, topk_idx, axis=1)
            topk_w = topk_w / (jnp.sum(topk_w, axis=-1, keepdims=True) + 1e-20)
            topk_w = topk_w * ROUTED_SCALE
            rw = jnp.zeros((T, E), dtype=scores.dtype).at[jnp.arange(T)[:, None], topk_idx].add(topk_w)
            return rw

        def _mlp(x, gw, uw, dw):
            return jax.nn.silu(x @ gw.T) * (x @ uw.T) @ dw.T
        B, S, _ = hidden_states.shape
        x = hidden_states.reshape(B * S, H)
        rw = _route(x, gate_w, gate_bias)
        expert_out = jax.vmap(lambda gw_, uw_, dw_: _mlp(x, gw_, uw_, dw_))(Wg, Wu, Wd)
        routed = jnp.einsum('eth,te->th', expert_out, rw)
        shared = _mlp(x, Sg, Su, Sd)
        out = (routed + shared).reshape(B, S, H)
        return out
    x = x + jnp.tanh(g_xattn[0]) * _L0_xattn_ref(_layernorm(x, axis=-1), ctx_1024, ctx_1024, mask_Bx1xSxS2_bf0, 0, L0_xattn_wq_w, L0_xattn_wq_b, L0_xattn_wk_w, L0_xattn_wk_b, L0_xattn_wv_w, L0_xattn_wv_b, L0_xattn_wo_w, L0_xattn_wo_b, L0_xattn_ln_g, L0_xattn_ln_b)
    x = x + jnp.tanh(g_ffn[0]) * _L0_ffn_ref(_layernorm(x, axis=-1), L0_ffn_w_gate, L0_ffn_w_up, L0_ffn_w_down)
    x = x + jnp.tanh(g_xattn[1]) * _L1_xattn_ref(_layernorm(x, axis=-1), ctx_1024, ctx_1024, L1_xattn_Wq, L1_xattn_bq, L1_xattn_Wk, L1_xattn_bk, L1_xattn_Wv, L1_xattn_bv, L1_xattn_Wo, L1_xattn_bo)
    x = x + jnp.tanh(g_ffn[1]) * _L1_ffn_ref(_layernorm(x, axis=-1), L1_ffn_gate_w, L1_ffn_gate_bias, L1_ffn_Wg, L1_ffn_Wu, L1_ffn_Wd, L1_ffn_Sg, L1_ffn_Su, L1_ffn_Sd)
    return x

_drawn_inputs = setup_inputs


def setup_inputs(seed=0):
    import zlib

    import numpy as np

    out = dict(_drawn_inputs(seed))
    spreads = {'g_ffn': (-1.0, 0.6),
     'L0_xattn_wq_b': (0.0, 0.1),
     'L0_xattn_wk_b': (0.0, 0.1),
     'L0_xattn_wv_b': (0.0, 0.1),
     'L0_xattn_wo_b': (0.0, 0.711),
     'L0_xattn_ln_g': (1.0, 0.2),
     'L0_xattn_ln_b': (0.0, 0.1)}
    factors = {'L1_xattn_Wq': 8.0,
     'L1_xattn_bq': 8.0,
     'L1_xattn_Wk': 8.0,
     'L1_xattn_bk': 64.0,
     'L1_xattn_Wv': 8.0,
     'L1_xattn_bv': 64.0,
     'L1_xattn_Wo': 8.0,
     'L1_xattn_bo': 64.0,
     'L1_ffn_gate_w': 48.161,
     'L1_ffn_gate_bias': 53.506,
     'L1_ffn_Wg': 48.633,
     'L1_ffn_Wu': 42.555,
     'L1_ffn_Wd': 42.586,
     'L1_ffn_Sg': 30.708,
     'L1_ffn_Su': 26.834,
     'L1_ffn_Sd': 26.633}
    for name, (base, spread) in spreads.items():
        noise = np.random.default_rng([zlib.crc32(name.encode()), seed]).standard_normal(out[name].shape)
        drawn = base * np.exp(spread * noise) if base else spread * noise
        out[name] = jnp.asarray(drawn.astype(out[name].dtype))
    for name, factor in factors.items():
        out[name] = (out[name] * factor).astype(out[name].dtype)
    return out
```

```python
from contextlib import ExitStack

import concourse.bass as bass
from concourse import mybir

F32 = mybir.dt.float32
F32R = mybir.dt.float32r
I32 = mybir.dt.int32
U8 = mybir.dt.uint8
U32 = mybir.dt.uint32
ACT = mybir.ActivationFunctionType
ALU = mybir.AluOpType
AX_X = mybir.AxisListType.X

P = 128
T = 2048
D = 256
NT = T // P
DC = D // P
S2 = 1601
KT = -(-S2 // P)
SK = KT * P
LAST = S2 - (KT - 1) * P
NH = 16
HD = D // NH
EPS = 1e-5
BLK = 512
NB = T // BLK
HIDDEN = 768


class Steps:

    def __init__(self, eng, sem, base=0):
        self.eng, self.sem, self.base, self.n = eng, sem, base, 0

    def inc(self, ins):
        ins.then_inc(self.sem, 1)
        self.n += 1

    def wait(self):
        self.eng.wait_ge(self.sem, self.base + self.n)


class Core:

    def __init__(self, nc, ctx):
        self.nc, self.ctx = nc, ctx

    def sb(self, name, shape, dt=F32):
        return self.ctx.enter_context(self.nc.sbuf_tensor(name, shape, dt))

    def sem(self, name):
        return self.ctx.enter_context(self.nc.semaphore(name))


def l0_attention(nc, a, weights):
    X, XN, bank = a["X"], a["XN"], a["bank"]
    ident, gates = a["ident"], a["gates"]
    with ExitStack() as ctx:
        k = Core(nc, ctx)
        C = k.sb("ctx_rows", [P, KT, D + 1])
        WKV = k.sb("w_kv", [P, DC, 2 * D])
        wkv_b = k.sb("w_kv_bias", [1, 2 * D])
        WQ = k.sb("w_q", [P, DC, D])
        BQ = k.sb("b_q", [P, DC])
        WO = k.sb("w_o", [P, DC, D])
        bo = k.sb("b_o", [1, D])
        hm = k.sb("head_mask", [P, P])
        G = k.sb("moments", [P, DC, D + 1])
        g_row = k.sb("moments_row", [1, D + 1])
        T1 = k.sb("moments_k", [P, DC, D])
        t1_row = k.sb("moments_k_row", [1, D])
        M = k.sb("vk", [P, DC, P])
        B = k.sb("vk_o", [P, DC, D])
        A0 = k.sb("q_to_out", [P, DC, D])
        a0_row = k.sb("q_to_out_bias", [1, D])
        lng = k.sb("ln_g", [P, D])
        lnb = k.sb("ln_b", [P, D])
        MSK = k.sb("mask", [P, NT, 401], I32)
        mrow = k.sb("mask_any", [P, NT])
        nan = k.sb("mask_nan", [P, NT])
        one = k.sb("one", [1, P])
        ST = k.sb("ln_stats", [P, NT, 6])
        MV = k.sb("ln_mv", [P, NT, 2])
        var = k.sb("ln_var", [P, NT])
        tmp = k.sb("ln_tmp", [P, NT])
        rt = k.sb("ln_root", [P, NT])
        rs = k.sb("ln_rstd", [P, NT])
        XT = k.sb("xn_t", [P, DC, T])
        Y = XN
        loaded_x = k.sem("l0_loaded_x")
        loaded_c = k.sem("l0_loaded_c")
        loaded_w = k.sem("l0_loaded_w")
        loaded_m = k.sem("l0_loaded_m")
        pad_ready = k.sem("l0_pad_ready")
        ones_ready = k.sem("l0_ones_ready")
        var_ready = k.sem("l0_var_ready")
        sqrt_ready = k.sem("l0_sqrt_ready")
        xn_ready = k.sem("l0_xn_ready")
        xt_ps = k.sem("l0_xt_ps")
        xt_ready = k.sem("l0_xt_ready")
        pe_step = k.sem("l0_pe_step")
        small_copied = k.sem("l0_small_copied")
        m_ready = k.sem("l0_m_ready")
        o_ready = k.sem("l0_o_ready")
        o_used = k.sem("l0_o_used")
        vstep = k.sem("l0_vstep")
        pool_step = k.sem("l0_pool_step")
        with nc.Block() as block:
            @block.sync
            def _(sp):
                sp.dma_start(X[:], a["x"].rearrange("a (n p) d -> p (a n) d", p=P)).then_inc(loaded_x, 16)
                ctx_d = a["ctx"]
                sp.dma_start(C[:, 0:KT - 1, 0:D],
                             ctx_d[0:(KT - 1) * P, :].rearrange("(n p) d -> p n d", p=P)).then_inc(loaded_c, 16)
                sp.dma_start(C[0:LAST, KT - 1, 0:D], ctx_d[(KT - 1) * P:S2, :]).then_inc(loaded_c, 16)
                sp.wait_ge(pad_ready, 1)
                sp.dma_start(MSK[:].bitcast(U8)[:, :, 0:S2],
                             a["mask"].rearrange("(n p) s -> p n s", p=P)).then_inc(loaded_m, 16)
                for w in weights:
                    w.load(sp)

            @block.scalar
            def _(s):
                s.dma_start(ident[:], a["ident_d"]).then_inc(loaded_w, 16)
                s.dma_start(WKV[:], a["w0kv"][0:D, :].rearrange("(c p) n -> p c n", p=P)).then_inc(loaded_w, 16)
                s.dma_start(wkv_b[:], a["w0kv"][D:D + 1, :]).then_inc(loaded_w, 16)
                s.dma_start(WQ[:], a["w0q"].rearrange("(c p) n -> p c n", p=P)).then_inc(loaded_w, 16)
                s.dma_start(BQ[:], a["b0q"]).then_inc(loaded_w, 16)
                s.dma_start(WO[:], a["w0o"].rearrange("(c p) n -> p c n", p=P)).then_inc(loaded_w, 16)
                s.dma_start(bo[:], a["b0o"].rearrange("(o n) -> o n", o=1)).then_inc(loaded_w, 16)
                s.dma_start(hm[:], a["head_mask_d"]).then_inc(loaded_w, 16)
                s.dma_start(lng[:], a["ln_g"].partition_broadcast(P)).then_inc(loaded_w, 16)
                s.dma_start(lnb[:], a["ln_b"].partition_broadcast(P)).then_inc(loaded_w, 16)
                s.dma_start(gates[:], a["gates_d"].partition_broadcast(P)).then_inc(loaded_w, 16)
                s.wait_ge(loaded_w, 11 * 16)
                s.activation(gates[:], gates[:], ACT.Tanh).then_inc(pool_step, 1)
                s.wait_ge(var_ready, 1)
                s.activation(rt[:], var[:], ACT.Sqrt).then_inc(sqrt_ready, 1)
                s.wait_ge(pe_step, 1)
                for i in range(DC):
                    s.copy(G[:, i, :], bank[i][:, 0:D + 1]).then_inc(small_copied, 1)
                s.copy(g_row[:], bank[2][0:1, 0:D + 1]).then_inc(small_copied, 1)
                s.wait_ge(pe_step, 2)
                for i in range(DC):
                    s.copy(T1[:, i, :], bank[3 + i][:, 0:D]).then_inc(small_copied, 1)
                s.copy(t1_row[:], bank[5][0:1, 0:D]).then_inc(small_copied, 1)
                s.wait_ge(pe_step, 4)
                for i in range(DC):
                    s.copy(B[:, i, :], bank[3 + i][:, 0:D]).then_inc(small_copied, 1)
                s.wait_ge(pe_step, 5)
                for i in range(DC):
                    s.copy(A0[:, i, :], bank[i][:, 0:D]).then_inc(small_copied, 1)
                s.copy(a0_row[:], bank[2][0:1, 0:D]).then_inc(small_copied, 1)
                for g in range(NB * DC):
                    s.wait_ge(xt_ps, g + 1)
                    s.copy(XT[:, g % DC, (g // DC) * BLK:(g // DC + 1) * BLK], bank[6 + g % 2][:]).then_inc(xt_ready, 1)
                s.wait_ge(var_ready, 2)
                s.activation(rt[:], var[:], ACT.Sqrt).then_inc(sqrt_ready, 1)

            @block.gpsimd
            def _(g):
                g.memset(MSK[:, :, 400:401], 0).then_inc(pad_ready, 1)
                g.memset(C[:, :, D:D + 1], 1.0).then_inc(ones_ready, 1)
                g.memset(one[:], 1.0).then_inc(ones_ready, 1)
                g.wait_ge(loaded_w, 11 * 16)
                g.wait_ge(pool_step, 1)
                g.tensor_scalar(lng[:], lng[:], gates[:, 0:1], None, ALU.mult).then_inc(pool_step, 1)
                g.tensor_scalar(lnb[:], lnb[:], gates[:, 0:1], None, ALU.mult).then_inc(pool_step, 1)
                g.wait_ge(pool_step, 3)
                g.wait_ge(xn_ready, NT)
                for t in range(NT):
                    g.tensor_tensor(X[:, t, :], X[:, t, :], lnb[:], ALU.add).then_inc(pool_step, 1)
                for w in weights:
                    w.split(g)

            @block.tensor
            def _(pe):
                pe.wait_ge(ones_ready, 2)
                pe.wait_ge(loaded_c, 32)
                for s in range(KT):
                    n = P if s < KT - 1 else LAST
                    for i in range(DC + 1):
                        m = P if i < DC else 1
                        last = pe.matmul(bank[i][0:m, 0:D + 1], C[0:n, s, i * P:i * P + m], C[0:n, s, :],
                                         start=s == 0, stop=s == KT - 1)
                last.then_inc(pe_step, 1)
                pe.wait_ge(loaded_w, 11 * 16)
                pe.wait_ge(small_copied, DC + 1)
                for i in range(DC + 1):
                    m = P if i < DC else 1
                    for j in range(DC):
                        pe.matmul(bank[3 + i][0:m, 0:D], G[:, j, i * P:i * P + m], WKV[:, j, 0:D],
                                  start=j == 0, stop=False)
                    last = pe.matmul(bank[3 + i][0:m, 0:D], g_row[:, i * P:i * P + m], wkv_b[:, 0:D],
                                     start=False, stop=True)
                last.then_inc(pe_step, 1)
                pe.wait_ge(small_copied, 2 * (DC + 1))
                for i in range(DC):
                    cols = slice(i * P, (i + 1) * P)
                    vcols = slice(D + i * P, D + (i + 1) * P)
                    for j in range(DC):
                        pe.matmul(bank[i][:, 0:P], WKV[:, j, vcols], T1[:, j, cols], start=j == 0, stop=False)
                    last = pe.matmul(bank[i][:, 0:P], wkv_b[:, vcols], t1_row[:, cols], start=False, stop=True)
                last.then_inc(pe_step, 1)
                pe.wait_ge(m_ready, DC)
                for i in range(DC):
                    last = pe.matmul(bank[3 + i][:, 0:D], M[:, i, :], WO[:, i, :], start=True, stop=True)
                last.then_inc(pe_step, 1)
                pe.wait_ge(small_copied, 2 * (DC + 1) + DC)
                for i in range(DC):
                    for j in range(DC):
                        pe.matmul(bank[i][:, 0:D], WQ[:, j, i * P:(i + 1) * P], B[:, j, :],
                                  start=j == 0, stop=j == DC - 1)
                for j in range(DC):
                    pe.matmul(bank[2][0:1, 0:D], BQ[:, j:j + 1], B[:, j, :], start=j == 0, stop=False)
                pe.matmul(bank[2][0:1, 0:D], one[:, 0:1], bo[:], start=False, stop=True).then_inc(pe_step, 1)
                for g in range(NB * DC):
                    pe.wait_ge(xn_ready, 4 * (g // DC) + 4)
                    if g >= 2:
                        pe.wait_ge(xt_ready, g - 1)
                    for q in range(4):
                        t = 4 * (g // DC) + q
                        last = pe.transpose(bank[6 + g % 2][:, q * P:(q + 1) * P],
                                            XN[:, t, (g % DC) * P:(g % DC + 1) * P], ident[:])
                    last.then_inc(xt_ps, 1)
                pe.wait_ge(small_copied, 3 * (DC + 1) + DC)
                for t in range(NT):
                    pe.wait_ge(xt_ready, DC * (t // 4) + DC)
                    if t >= 4:
                        pe.wait_ge(o_used, t - 3)
                    b = bank[2 + t % 4]
                    for j in range(DC):
                        pe.matmul(b[:, 0:D], XT[:, j, t * P:(t + 1) * P], A0[:, j, :], start=j == 0, stop=False)
                    pe.matmul(b[:, 0:D], one[:], a0_row[:], start=False, stop=True).then_inc(o_ready, 1)

            @block.vector
            def _(v):
                st = Steps(v, vstep)
                v.wait_ge(loaded_x, 16)

                def stats(src):
                    for t in range(NT):
                        st.inc(v.bn_stats(ST[:, t, :], src[:, t, :]))
                    st.wait()
                    for t in range(NT):
                        st.inc(v.bn_aggr(MV[:, t, :], ST[:, t, :]))
                    st.wait()

                def rstd(n):
                    st.inc(v.tensor_scalar(var[:], MV[:, :, 1], EPS, None, ALU.add))
                    st.wait()
                    v.tensor_copy(tmp[:], var[:]).then_inc(var_ready, 1)
                    v.wait_ge(sqrt_ready, n)
                    v.wait_ge(var_ready, n)
                    dve_newton(v, st, rs, rt, var, tmp)

                stats(X)
                rstd(1)
                for t in range(NT):
                    v.tensor_scalar(XN[:, t, :], X[:, t, :], MV[:, t, 0:1], rs[:, t:t + 1],
                                    ALU.subtract, ALU.mult).then_inc(xn_ready, 1)
                v.wait_ge(pe_step, 3)
                for i in range(DC):
                    v.tensor_tensor(M[:, i, :], bank[i][:, 0:P], hm[:], ALU.mult).then_inc(m_ready, 1)
                v.wait_ge(loaded_m, 16)
                st.inc(v.tensor_reduce(mrow[:], MSK[:], AX_X, ALU.max))
                st.wait()
                st.inc(v.tensor_scalar(nan[:], mrow[:], 0.0, 3e38, ALU.is_gt, ALU.mult))
                st.wait()
                st.inc(v.tensor_scalar(nan[:], nan[:], 10.0, None, ALU.mult))
                st.wait()
                st.inc(v.tensor_tensor(nan[:], nan[:], nan[:], ALU.subtract))
                for t in range(NT):
                    v.wait_ge(o_ready, t + 1)
                    v.tensor_tensor(Y[:, t, :], bank[2 + t % 4][:, 0:D], XN[:, t, :], ALU.add).then_inc(o_used, 1)
                v.wait_ge(o_used, NT)
                stats(Y)
                rstd(2)
                st.inc(v.tensor_tensor(rs[:], rs[:], nan[:], ALU.add))
                st.wait()
                for t in range(NT):
                    st.inc(v.tensor_scalar(Y[:, t, :], Y[:, t, :], MV[:, t, 0:1], rs[:, t:t + 1],
                                           ALU.subtract, ALU.mult))
                st.wait()
                v.wait_ge(pool_step, 3 + NT)
                for t in range(NT):
                    st.inc(v.tensor_tensor(Y[:, t, :], Y[:, t, :], lng[:], ALU.mult))
                st.wait()
                for t in range(NT):
                    st.inc(v.tensor_tensor(X[:, t, :], X[:, t, :], Y[:, t, :], ALU.add))
                st.wait()


def dve_newton(v, st, rs, rt, var, tmp):
    st.inc(v.reciprocal(rs[:], rt[:]))
    st.wait()
    st.inc(v.tensor_tensor(tmp[:], rs[:], rs[:], ALU.mult))
    st.wait()
    st.inc(v.tensor_tensor(tmp[:], tmp[:], var[:], ALU.mult))
    st.wait()
    st.inc(v.tensor_scalar(tmp[:], tmp[:], -0.5, 1.5, ALU.mult, ALU.add))
    st.wait()
    st.inc(v.tensor_tensor(rs[:], rs[:], tmp[:], ALU.mult))
    st.wait()


class Split:

    def __init__(self, c, name, shape, source, dt=F32):
        self.raw = c.sb(name + "_raw", shape, dt)
        self.hi = c.sb(name + "_hi", shape, F32R)
        self.lo = c.sb(name + "_lo", shape, F32R)
        self.dt = dt
        self.loaded = c.sem(name + "_loaded")
        self.cast = c.sem(name + "_cast")
        self.ready = c.sem(name + "_split")
        self.source = source
        full = sum(rows == source[0][0] for rows, _ in source)
        self.parts = [(source[0][0], slice(0, full))]
        if full < len(source):
            self.parts.append((source[-1][0], slice(full, full + 1)))

    def load(self, eng):
        self.n = 0
        for j, (rows, src) in enumerate(self.source):
            eng.dma_start(self.raw[0:rows, j, :], src).then_inc(self.loaded, 16)
            self.n += 16

    def split(self, eng):
        eng.wait_ge(self.loaded, 16 * len(self.source))
        for n, (rows, chunks) in enumerate(self.parts):
            raw = self.raw[0:rows, chunks, :]
            if self.dt != F32:
                raw = raw.bitcast(F32)
                eng.tensor_copy(raw, self.raw[0:rows, chunks, :]).then_inc(self.cast, 1)
                eng.wait_ge(self.cast, n + 1)
            hi, lo = self.hi[0:rows, chunks, :], self.lo[0:rows, chunks, :]
            eng.tensor_copy(hi, raw).then_inc(self.ready, 1)
            eng.wait_ge(self.ready, 2 * n + 1)
            eng.tensor_tensor(lo, raw, hi.bitcast(F32), ALU.subtract).then_inc(self.ready, 1)

    def wait(self, eng):
        eng.wait_ge(self.ready, 2 * len(self.parts))


def chunks_of(src, rows):
    return [(min(P, rows - r), src[r:min(r + P, rows), :]) for r in range(0, rows, P)]


class Norm:

    def __init__(self, k, a, name):
        self.a = a
        self.ST = k.sb(name + "_stats", [P, NT, 6])
        self.MV = k.sb(name + "_mv", [P, NT, 2])
        self.var = k.sb(name + "_var", [P, NT])
        self.tmp = k.sb(name + "_tmp", [P, NT])
        self.rt = k.sb(name + "_root", [P, NT])
        self.rs = k.sb(name + "_rstd", [P, NT])
        self.step = k.sem(name + "_step")
        self.var_ready = k.sem(name + "_var_ready")
        self.sqrt_ready = k.sem(name + "_sqrt_ready")
        self.xn_ready = k.sem(name + "_xn_ready")
        self.xt_ps = k.sem(name + "_xt_ps")
        self.hi_ready = k.sem(name + "_hi_ready")
        self.lo_ready = k.sem(name + "_lo_ready")

    def vector(self, v):
        a, st = self.a, Steps(v, self.step)
        X, XN = a["X"], a["XN"]
        for t in range(NT):
            st.inc(v.bn_stats(self.ST[:, t, :], X[:, t, :]))
        st.wait()
        for t in range(NT):
            st.inc(v.bn_aggr(self.MV[:, t, :], self.ST[:, t, :]))
        st.wait()
        v.tensor_scalar(self.var[:], self.MV[:, :, 1], EPS, None, ALU.add).then_inc(self.var_ready, 1)
        v.wait_ge(self.sqrt_ready, 1)
        dve_newton(v, st, self.rs, self.rt, self.var, self.tmp)
        for t in range(NT):
            v.tensor_scalar(XN[:, t, :], X[:, t, :], self.MV[:, t, 0:1], self.rs[:, t:t + 1],
                            ALU.subtract, ALU.mult).then_inc(self.xn_ready, 1)
        for g in range(NB * DC):
            b, j = divmod(g, DC)
            v.wait_ge(self.hi_ready, g + 1)
            v.tensor_tensor(a["xt_lo"][:, j, b * BLK:(b + 1) * BLK], a["bank"][6 + g % 2][:],
                            a["xt_hi"][:, j, b * BLK:(b + 1) * BLK].bitcast(F32), ALU.subtract).then_inc(self.lo_ready, 1)

    def scalar(self, s):
        a = self.a
        s.wait_ge(self.var_ready, 1)
        s.activation(self.rt[:], self.var[:], ACT.Sqrt).then_inc(self.sqrt_ready, 1)
        for g in range(NB * DC):
            b, j = divmod(g, DC)
            s.wait_ge(self.xt_ps, g + 1)
            s.copy(a["xt_hi"][:, j, b * BLK:(b + 1) * BLK], a["bank"][6 + g % 2][:]).then_inc(self.hi_ready, 1)

    def tensor(self, pe):
        a = self.a
        for g in range(NB * DC):
            b, j = divmod(g, DC)
            pe.wait_ge(self.xn_ready, 4 * b + 4)
            if g >= 2:
                pe.wait_ge(self.lo_ready, g - 1)
            for q in range(4):
                last = pe.transpose(a["bank"][6 + g % 2][:, q * P:(q + 1) * P],
                                    a["XN"][:, 4 * b + q, j * P:(j + 1) * P], a["ident"][:])
            last.then_inc(self.xt_ps, 1)


def products(pe, out, lhs, rhs, start, stop):
    (lh, ll), (rh, rl) = lhs, rhs
    pe.matmul(out, lh, rh, start=start, stop=False)
    pe.matmul(out, lh, rl, start=False, stop=False)
    return pe.matmul(out, ll, rh, start=False, stop=stop)


class Ffn:

    def __init__(self, k, a, name, w1, w2, hidden, scale, evacuate, low_on_vector=False):
        self.a, self.w1, self.w2, self.hidden, self.scale, self.evacuate = a, w1, w2, hidden, scale, evacuate
        self.low_on_vector = low_on_vector
        self.sizes = [min(P, hidden - r) for r in range(0, hidden, P)]
        self.n = len(self.sizes)
        self.sg = k.sb(name + "_silu", [P, 2, BLK])
        self.hf = k.sb(name + "_h", [P, 2, BLK])
        self.hh = k.sb(name + "_h_hi", [P, self.n, BLK], F32R)
        self.hl = k.sb(name + "_h_lo", [P, self.n, BLK], F32R)
        self.gu_ready = k.sem(name + "_gu_ready")
        self.silu_ready = k.sem(name + "_silu_ready")
        self.h_ready = k.sem(name + "_h_ready")
        self.hl_ready = k.sem(name + "_hl_ready")
        self.down_done = k.sem(name + "_down_done")
        self.hh_ready = k.sem(name + "_hh_ready")
        self.out_used = k.sem(name + "_out_used")

    def reuse(self, i, c):
        dist = 1 if c == 0 and self.n % 2 else 2
        return i * self.n + c - dist + 3

    def tensor(self, pe, norm):
        a, n = self.a, self.n
        for w in (self.w1, self.w2):
            w.wait(pe)
        with pe.Fori(0, NB) as i:
            pe.wait_ge(norm.lo_ready, i * DC + DC)
            toks = bass.ts(i, BLK)
            for c, m in enumerate(self.sizes):
                pe.wait_ge(self.h_ready, self.reuse(i, c))
                for part in range(2):
                    cols = slice(part * self.hidden + c * P, part * self.hidden + c * P + m)
                    out = a["bank"][2 * (c % 2) + part][0:m, :]
                    for j in range(DC):
                        last = products(pe, out, (self.w1.hi[:, j, cols], self.w1.lo[:, j, cols]),
                                        (a["xt_hi"][:, j, toks], a["xt_lo"][:, j, toks]),
                                        start=j == 0, stop=j == DC - 1)
                last.then_inc(self.gu_ready, 1)
            pe.wait_ge(self.out_used, i * 4 + 4)
            for c, m in enumerate(self.sizes):
                pe.wait_ge(self.hl_ready, i * n + c + 1 + 2)
                for q in range(4):
                    tok = slice(q * P, (q + 1) * P)
                    last = products(pe, a["bank"][4 + q][:, 0:D], (self.hh[0:m, c, tok], self.hl[0:m, c, tok]),
                                    (self.w2.hi[0:m, c, :], self.w2.lo[0:m, c, :]), start=c == 0, stop=c == n - 1)
                last.then_inc(self.down_done, 1)

    def scalar(self, s):
        n = self.n
        with s.Fori(0, NB) as i:
            for c in range(n + 1):
                if c < n:
                    m = self.sizes[c]
                    s.wait_ge(self.gu_ready, i * n + c + 1)
                    s.activation(self.sg[0:m, c % 2, :], self.a["bank"][2 * (c % 2)][0:m, :], ACT.Silu,
                                 scale=self.scale).then_inc(self.silu_ready, 1)
                if c >= 1:
                    m = self.sizes[c - 1]
                    s.wait_ge(self.h_ready, i * n + c + 2)
                    s.wait_ge(self.down_done, i * n + c)
                    s.copy(self.hh[0:m, c - 1, :], self.hf[0:m, (c - 1) % 2, :]).then_inc(self.hh_ready, 1)

    def vector(self, v):
        a, n = self.a, self.n
        v.sem_inc(self.h_ready, 2)
        if self.low_on_vector:
            self.credits(v)
        with v.Fori(0, NB) as i:
            for c in range(n + 1):
                if c < n:
                    m = self.sizes[c]
                    v.wait_ge(self.silu_ready, i * n + c + 1)
                    v.wait_ge(self.hl_ready, self.reuse(i, c))
                    v.tensor_tensor(self.hf[0:m, c % 2, :], self.sg[0:m, c % 2, :],
                                    a["bank"][2 * (c % 2) + 1][0:m, :], ALU.mult).then_inc(self.h_ready, 1)
                if self.low_on_vector and c >= 1:
                    self.low(v, i, c - 1)
            v.wait_ge(self.down_done, i * n + n + n)
            for q in range(4):
                self.evacuate(v, i * 4 + q, a["bank"][4 + q][:, 0:D]).then_inc(self.out_used, 1)

    def credits(self, eng):
        eng.sem_inc(self.hl_ready, 2)
        eng.sem_inc(self.down_done, self.n)
        eng.sem_inc(self.out_used, 4)

    def low(self, eng, i, c):
        m = self.sizes[c]
        eng.wait_ge(self.hh_ready, i * self.n + c + 1)
        eng.tensor_tensor(self.hl[0:m, c, :], self.hf[0:m, c % 2, :], self.hh[0:m, c, :].bitcast(F32),
                          ALU.subtract).then_inc(self.hl_ready, 1)

    def gpsimd(self, g):
        self.credits(g)
        with g.Fori(0, NB) as i:
            for c in range(self.n):
                self.low(g, i, c)


def l0_ffn(nc, a, w1, w2):
    with ExitStack() as ctx:
        k = Core(nc, ctx)
        norm = Norm(k, a, "n1")
        coef = k.sb("ffn0_coef", [P, 1])
        coef_ready = k.sem("ffn0_coef_ready")

        def residual(v, t, ps):
            x = a["X"][:, bass.ds(t, 1), :].rearrange("p a d -> p (a d)")
            return v.scalar_tensor_tensor(x, ps, coef[:], x, ALU.mult, ALU.add)

        ffn = Ffn(k, a, "ffn0", w1, w2, HIDDEN, 1 / 127, residual)
        with nc.Block() as block:
            @block.tensor
            def _(pe):
                norm.tensor(pe)
                pe.wait_ge(norm.lo_ready, NB * DC)
                ffn.tensor(pe, norm)

            @block.scalar
            def _(s):
                norm.scalar(s)
                ffn.scalar(s)

            @block.vector
            def _(v):
                norm.vector(v)
                v.wait_ge(coef_ready, 1)
                ffn.vector(v)

            @block.gpsimd
            def _(g):
                g.tensor_scalar(coef[:], a["gates"][:, 1:2], 1 / 127 ** 2, None, ALU.mult).then_inc(coef_ready, 1)
                ffn.gpsimd(g)


class Turn:

    def __init__(self, k, a, name):
        self.a = a
        self.xt_ps = k.sem(name + "_xt_ps")
        self.hi_ready = k.sem(name + "_hi_ready")
        self.lo_ready = k.sem(name + "_lo_ready")

    def vector(self, v):
        a = self.a
        for g in range(NB * DC):
            b, j = divmod(g, DC)
            v.wait_ge(self.hi_ready, g + 1)
            v.tensor_tensor(a["xt_lo"][:, j, b * BLK:(b + 1) * BLK], a["bank"][6 + g % 2][:],
                            a["xt_hi"][:, j, b * BLK:(b + 1) * BLK].bitcast(F32), ALU.subtract).then_inc(self.lo_ready, 1)

    def scalar(self, s):
        a = self.a
        for g in range(NB * DC):
            b, j = divmod(g, DC)
            s.wait_ge(self.xt_ps, g + 1)
            s.copy(a["xt_hi"][:, j, b * BLK:(b + 1) * BLK], a["bank"][6 + g % 2][:]).then_inc(self.hi_ready, 1)

    def tensor(self, pe):
        a = self.a
        for g in range(NB * DC):
            b, j = divmod(g, DC)
            if g >= 2:
                pe.wait_ge(self.lo_ready, g - 1)
            for q in range(4):
                last = pe.transpose(a["bank"][6 + g % 2][:, q * P:(q + 1) * P],
                                    a["XN"][:, 4 * b + q, j * P:(j + 1) * P], a["ident"][:])
            last.then_inc(self.xt_ps, 1)


VW = HD + 1


def l1_projections(nc, a, VA, q_d, k_d):
    with ExitStack() as ctx:
        k = Core(nc, ctx)
        norm = Norm(k, a, "n2")
        W = Split(k, "l1_w", [P, DC, 3 * D], chunks_of(a["w1qkv"], D))
        CT = Split(k, "ctx_t", [P, DC, SK], chunks_of(a["ctx_t"], D))
        b_qk = k.sb("b_qk", [P, 2 * DC])
        b_v = k.sb("b_v", [1, D])
        one = k.sb("one1", [1, P])
        full = k.sb("qk_full", [P, 2, BLK])
        hi = k.sb("qk_hi", [P, 2, BLK], F32R)
        lo = k.sb("qk_lo", [P, 2, BLK], F32R)
        loaded = k.sem("p1_loaded")
        set_ready = k.sem("p1_set_ready")
        qk_ps = k.sem("p1_qk_ps")
        full_ready = k.sem("p1_full_ready")
        hi_ready = k.sem("p1_hi_ready")
        lo_ready = k.sem("p1_lo_ready")
        hi_out = [k.sem(f"p1_hi_out{i}") for i in range(2)]
        lo_out = [k.sem(f"p1_lo_out{i}") for i in range(2)]
        v_ps = k.sem("p1_v_ps")
        v_ready = k.sem("p1_v_ready")
        pieces = [(D + m * P, CT, n, min(BLK, SK - n), k_d, m) for m in range(DC) for n in range(0, SK, BLK)]
        nk = len(pieces)
        pieces += [(m * P, None, n, BLK, q_d, m) for n in range(0, T, BLK) for m in range(DC)]
        with nc.Block() as block:
            @block.sync
            def _(sp):
                W.load(sp)
                CT.load(sp)
                sp.dma_start(b_qk[:], a["b1qk"]).then_inc(loaded, 16)
                sp.dma_start(b_v[:], a["b1v"].rearrange("(o n) -> o n", o=1)).then_inc(loaded, 16)
                for n, (_, _, c0, w, dram, m) in enumerate(pieces):
                    sp.wait_ge(hi_ready, n + 1)
                    sp.dma_start(dram[0][m * P:(m + 1) * P, c0:c0 + w], hi[:, n % 2, 0:w].bitcast(F32)).then_inc(hi_out[n % 2], 16)
                    sp.wait_ge(lo_ready, n + 1)
                    sp.dma_start(dram[1][m * P:(m + 1) * P, c0:c0 + w], lo[:, n % 2, 0:w].bitcast(F32)).then_inc(lo_out[n % 2], 16)
                for n in range(2):
                    sp.wait_ge(hi_out[n], 8 * len(pieces))
                    sp.wait_ge(lo_out[n], 8 * len(pieces))

            @block.tensor
            def _(pe):
                def piece(n):
                    w0, src, c0, w, _, _ = pieces[n]
                    if n >= 2:
                        pe.wait_ge(full_ready, n - 1)
                    for j in range(DC):
                        rhs = (src.hi[:, j, c0:c0 + w], src.lo[:, j, c0:c0 + w]) if src else \
                            (a["xt_hi"][:, j, c0:c0 + w], a["xt_lo"][:, j, c0:c0 + w])
                        last = products(pe, a["bank"][n % 2][:, 0:w],
                                        (W.hi[:, j, w0:w0 + P], W.lo[:, j, w0:w0 + P]), rhs,
                                        start=j == 0, stop=j == DC - 1)
                    last.then_inc(qk_ps, 1)

                norm.tensor(pe)
                W.wait(pe)
                CT.wait(pe)
                pe.wait_ge(loaded, 32)
                pe.wait_ge(set_ready, 2)
                for n in range(nk):
                    piece(n)
                for s in range(KT):
                    if s >= 4:
                        pe.wait_ge(v_ready, s - 3)
                    b = a["bank"][2 + s % 4][:, 0:D]
                    keys = slice(s * P, (s + 1) * P)
                    for j in range(DC):
                        products(pe, b, (CT.hi[:, j, keys], CT.lo[:, j, keys]),
                                 (W.hi[:, j, 2 * D:3 * D], W.lo[:, j, 2 * D:3 * D]), start=j == 0, stop=False)
                    pe.matmul(b, one[:], b_v[:], start=False, stop=True).then_inc(v_ps, 1)
                pe.wait_ge(norm.lo_ready, NB * DC)
                for n in range(nk, len(pieces)):
                    piece(n)

            @block.scalar
            def _(s):
                norm.scalar(s)
                s.wait_ge(loaded, 32)
                for n, (w0, _, _, w, _, m) in enumerate(pieces):
                    s.wait_ge(qk_ps, n + 1)
                    if n >= 2:
                        s.wait_ge(lo_ready, n - 1)
                        s.wait_ge(hi_out[n % 2], 16 * (n // 2))
                    bias = b_qk[:, (DC if n < nk else 0) + m:(DC if n < nk else 0) + m + 1]
                    s.activation(full[:, n % 2, 0:w], a["bank"][n % 2][:, 0:w], ACT.Identity,
                                 bias=bias).then_inc(full_ready, 1)
                    s.wait_ge(full_ready, n + 1)
                    s.copy(hi[:, n % 2, 0:w], full[:, n % 2, 0:w]).then_inc(hi_ready, 1)

            @block.gpsimd
            def _(g):
                g.memset(one[:], 1.0).then_inc(set_ready, 1)
                g.memset(VA[:, KT - 1], 0.0).then_inc(set_ready, 1)
                W.split(g)
                CT.split(g)
                for n, (_, _, _, w, _, _) in enumerate(pieces):
                    g.wait_ge(hi_ready, n + 1)
                    if n >= 2:
                        g.wait_ge(lo_out[n % 2], 16 * (n // 2))
                    g.tensor_tensor(lo[:, n % 2, 0:w], full[:, n % 2, 0:w], hi[:, n % 2, 0:w].bitcast(F32),
                                    ALU.subtract).then_inc(lo_ready, 1)

            @block.vector
            def _(v):
                norm.vector(v)
                v.wait_ge(set_ready, 2)
                v.memset(VA[:, 0:KT - 1, :, HD:VW], 1.0)
                v.memset(VA[0:LAST, KT - 1, :, HD:VW], 1.0)
                for s in range(KT):
                    n = P if s < KT - 1 else LAST
                    v.wait_ge(v_ps, s + 1)
                    v.tensor_copy(VA[0:n, s, :, 0:HD],
                                  a["bank"][2 + s % 4][0:n, 0:D].rearrange("p (h d) -> p h d", h=NH)).then_inc(v_ready, 1)


NE = NT * 2
KW = 402
SC = NB * KT
ROW_M = 96


def l1_attention(nc, a, VA, q_d, k_d, clear):
    bank, ON = a["bank"], a["XN"]
    with ExitStack() as ctx:
        k = Core(nc, ctx)
        QS = [k.sb(f"q_stack{i}", [P, T], F32R) for i in range(2)]
        KS = [k.sb(f"k_stack{i}", [P, SK], F32R) for i in range(2)]
        VH = [k.sb(f"v_head{i}", [P, KT, 32]) for i in range(2)]
        PB = [k.sb(f"probs{i}", [P, T]) for i in range(3)]
        mx = k.sb("row_max2", [P, NT, 2])
        mneg = k.sb("row_max_neg", [P, NT])
        MR = k.sb("max_row", [NT, P], F32R)
        OS = k.sb("out_sum", [P, BLK])
        rec = k.sb("recip", [P, 4, NB, 1])
        zero_ready = k.sem("a_zero_ready")
        stack_loaded = k.sem("a_stack_loaded")
        vh_ready = k.sem("a_vh_ready")
        mx_ready = k.sem("a_mx_ready")
        mx_used = k.sem("a_mx_used")
        mneg_ready = k.sem("a_mneg_ready")
        misc_ready = k.sem("a_misc_ready")
        mr_ready = k.sem("a_mr_ready")
        mrow_loaded = k.sem("a_mrow_loaded")
        score_ready = k.sem("a_score_ready")
        exp_ready = k.sem("a_exp_ready")
        pv_done = k.sem("a_pv_done")
        os_ready = k.sem("a_os_ready")
        on_ready = k.sem("a_on_ready")
        step = k.sem("a_step")
        vh_zero = k.sem("a_vh_zero")
        carrier = k.sem("a_wait_carrier")
        set_step = k.sem("a_set_step")

        def load_stack(sp, h, p):
            for dst, (hi_d, lo_d), lo_rows, cols in ((QS[p], q_d, (64,), T), (KS[p], k_d, (32,), SK)):
                for r in (0, 32, 64):
                    src = lo_d if r in lo_rows else hi_d
                    sp.dma_start(dst[r:r + HD, :].bitcast(F32), src[bass.ds(h * HD, HD), :]).then_inc(stack_loaded, 16)

        def put_max(sp, n, p):
            sp.wait_ge(mr_ready, n + 1)
            sp.dma_start(QS[p][ROW_M:ROW_M + 1, :].bitcast(F32).rearrange("o (t q) -> o t q", q=P),
                         MR[:].bitcast(F32)).then_inc(mrow_loaded, 16)

        def sp_window(sp, n, p, following):
            if following:
                sp.wait_ge(exp_ready, SC * n + 2)
                load_stack(sp, n + 1, 1 - p)
                for i in range(4):
                    clear.dma(sp, 4 * n + i + clear.total - 4 * (NH - 1))
                put_max(sp, n + 1, 1 - p)

        def pe_max(pe, n, p, e):
            t, half = divmod(e, 2)
            pe.wait_ge(mx_used, n * NE + e + 1)
            for b in range(2):
                key0 = (2 * half + b) * KW
                last = pe.matmul(bank[3 + 2 * (e % 2) + b][:, 0:KW], QS[p][0:ROW_M, t * P:(t + 1) * P],
                                 KS[p][0:ROW_M, key0:key0 + KW], start=True, stop=True)
            last.then_inc(mx_ready, 1)

        def pe_turn_max(pe, n, before):
            pe.wait_ge(mneg_ready, n + 1)
            if before:
                pe.wait_ge(on_ready, n)
            pe.transpose(bank[2][0:NT, 0:P], mneg[:], a["ident"][:]).then_inc(misc_ready, 1)

        def pe_window(pe, n, p, following):
            pe.wait_ge(mrow_loaded, 16 * (n + 1))
            pe.wait_ge(vh_ready, n + 1)
            if following:
                todo = list(range(NE))
            for c in range(KT + 1):
                if c < KT:
                    for qb in range(NB):
                        i = c * NB + qb
                        pe.wait_ge(exp_ready, SC * n + i + 1)
                        pe.matmul(bank[i % 2][:], KS[p][:, c * P:(c + 1) * P], QS[p][:, qb * BLK:(qb + 1) * BLK],
                                  start=True, stop=True).then_inc(score_ready, 1)
                        if following and c >= 1 and qb < 3 and todo:
                            if c == 1 and qb == 0:
                                pe.wait_ge(stack_loaded, 96 * (n + 2))
                            pe_max(pe, n + 1, 1 - p, todo.pop(0))
                if c >= 1:
                    j = c - 1
                    pe.wait_ge(exp_ready, SC * n + NB * c + 2)
                    for qb in range(NB):
                        last = pe.matmul(bank[7][32 * qb:32 * qb + 32, :], VH[p][:, j, :],
                                         PB[(j + p) % 3][:, qb * BLK:(qb + 1) * BLK],
                                         start=j == 0, stop=j == KT - 1)
                    last.then_inc(pv_done, 1)
                if following and c == KT - 1:
                    assert not todo
                    pe_turn_max(pe, n + 1, True)
            pe.wait_ge(os_ready, n + 1)
            if following:
                pe.wait_ge(mr_ready, n + 2)
            for s in range(4):
                last = pe.transpose(bank[2][:, s * P:(s + 1) * P], OS[:, s * P:(s + 1) * P], a["ident"][:])
            last.then_inc(misc_ready, 1)

        def act_window(s, n, p):
            for c in range(KT):
                dist = 2 if p == 0 and c < 2 else 3
                s.wait_ge(pv_done, n * KT + c + 1 - dist + 3)
                for qb in range(NB):
                    i = c * NB + qb
                    s.wait_ge(score_ready, SC * n + i + 1)
                    s.activation(PB[(c + p) % 3][:, qb * BLK:(qb + 1) * BLK], bank[i % 2][:], ACT.Exp,
                                 scale=1 / HD ** 0.5).then_inc(exp_ready, 1)

        def dve_max(v, n, first):
            for e in range(NE):
                v.wait_ge(mx_ready, n * NE + e + 1)
                b = 3 + 2 * (e % 2)
                v.tensor_reduce(mx[:, e // 2, e % 2:e % 2 + 1], a["banks"][:, b:b + 2, 0:KW],
                                mybir.AxisListType.XY, ALU.max).then_inc(mx_used, 1)
            v.wait_ge(mx_used, n * NE + NE + 2)
            v.tensor_reduce(mneg[:], mx[:], AX_X, ALU.max, negate=True).then_inc(mneg_ready, 1)
            v.wait_ge(misc_ready, 1 if first else 2 * n)
            if not first:
                v.wait_ge(mrow_loaded, 16 * n)
            v.tensor_copy(MR[:], bank[2][0:NT, 0:P]).then_inc(mr_ready, 1)

        def dve_window(v, n, following):
            if following:
                dve_max(v, n + 1, False)
            v.wait_ge(pv_done, (n + 1) * KT + 3)
            v.tensor_copy(OS[:], bank[7][:]).then_inc(os_ready, 1)
            v.wait_ge(misc_ready, 2 * n + (3 if following else 2))
            ps = bank[2][:].rearrange("p (s b r) -> p s b r", s=4, b=NB)
            v.reciprocal(rec[:], ps[:, :, :, HD:VW]).then_inc(step, 1)
            v.wait_ge(step, n + 1)
            v.tensor_tensor(ON[:, :, bass.ds(n * HD, HD)].rearrange("p (b s) d -> p s b d", s=4),
                            ps[:, :, :, 0:HD], rec[:].to_broadcast([P, 4, NB, HD]), ALU.mult).then_inc(on_ready, 1)

        def pool_vh(g, n, p, first):
            if not first:
                g.wait_ge(pv_done, 3 + KT * (n - 1))
                g.sem_inc(carrier, 1)
            g.tensor_copy(VH[p][:, :, 0:VW], VA[:, :, bass.ds(n, 1), :].rearrange("p k o d -> p k (o d)")).then_inc(vh_ready, 1)

        with nc.Block() as block:
            @block.sync
            def _(sp):
                sp.wait_ge(zero_ready, 1)
                load_stack(sp, 0, 0)
                sp.wait_ge(clear.ready, 1)
                for i in range(clear.total - 4 * (NH - 1)):
                    clear.dma(sp, i)
                put_max(sp, 0, 0)
                with sp.Fori(0, NH // 2 - 1) as i:
                    sp_window(sp, 2 * i, 0, True)
                    sp_window(sp, 2 * i + 1, 1, True)
                sp_window(sp, NH - 2, 0, True)
                sp.wait_ge(stack_loaded, 96 * NH)
                sp.wait_ge(mrow_loaded, 16 * NH)

            @block.tensor
            def _(pe):
                pe.wait_ge(stack_loaded, 96)
                for e in range(NE):
                    pe_max(pe, 0, 0, e)
                pe_turn_max(pe, 0, False)
                with pe.Fori(0, NH // 2 - 1) as i:
                    pe_window(pe, 2 * i, 0, True)
                    pe_window(pe, 2 * i + 1, 1, True)
                pe_window(pe, NH - 2, 0, True)
                pe_window(pe, NH - 1, 1, False)

            @block.scalar
            def _(s):
                with s.Fori(0, NH // 2) as i:
                    act_window(s, 2 * i, 0)
                    act_window(s, 2 * i + 1, 1)

            @block.vector
            def _(v):
                v.sem_inc(mx_used, 2)
                v.sem_inc(exp_ready, 2)
                v.sem_inc(pv_done, 3)
                v.sem_inc(on_ready, 1)
                for p in range(2):
                    v.memset(QS[p][:].bitcast(F32), 0.0)
                    v.memset(KS[p][:].bitcast(F32), 0.0).then_inc(set_step, 1)
                    v.wait_ge(set_step, p + 1)
                    last = v.memset(KS[p][ROW_M:P, :].bitcast(F32), 1.0)
                last.then_inc(zero_ready, 1)
                dve_max(v, 0, True)
                with v.Fori(0, NH // 2 - 1) as i:
                    dve_window(v, 2 * i, True)
                    dve_window(v, 2 * i + 1, True)
                dve_window(v, NH - 2, True)
                dve_window(v, NH - 1, False)

            @block.gpsimd
            def _(g):
                g.memset(clear.Z[:], 0.0).then_inc(clear.ready, 1)
                for p in range(2):
                    g.memset(VH[p][:], 0.0).then_inc(vh_zero, 1)
                g.wait_ge(vh_zero, 2)
                for p in range(2):
                    pool_vh(g, p, p, True)
                with g.Fori(0, NH // 2 - 1) as i:
                    pool_vh(g, 2 * i + 2, 0, False)
                    pool_vh(g, 2 * i + 3, 1, False)


def l1_output(nc, a):
    X, bank = a["X"], a["bank"]
    with ExitStack() as ctx:
        k = Core(nc, ctx)
        W = Split(k, "l1_wo", [P, DC, D], chunks_of(a["w1o"], D))
        turn = Turn(k, a, "l1_turn")
        bo = k.sb("b1o", [1, D])
        one = k.sb("one2", [1, P])
        loaded = k.sem("o1_loaded")
        one_ready = k.sem("o1_one_ready")
        o_ready = k.sem("o1_ready")
        o_used = k.sem("o1_used")
        with nc.Block() as block:
            @block.sync
            def _(sp):
                W.load(sp)
                sp.dma_start(bo[:], a["b1o"].rearrange("(o n) -> o n", o=1)).then_inc(loaded, 16)

            @block.gpsimd
            def _(g):
                g.memset(one[:], 1.0).then_inc(one_ready, 1)
                W.split(g)

            @block.scalar
            def _(s):
                turn.scalar(s)

            @block.tensor
            def _(pe):
                turn.tensor(pe)
                W.wait(pe)
                pe.wait_ge(loaded, 16)
                pe.wait_ge(one_ready, 1)
                for t in range(NT):
                    pe.wait_ge(turn.lo_ready, DC * (t // 4) + DC)
                    if t >= 4:
                        pe.wait_ge(o_used, t - 3)
                    ps = bank[2 + t % 4][:, 0:D]
                    tok = slice(t * P, (t + 1) * P)
                    for j in range(DC):
                        products(pe, ps, (a["xt_hi"][:, j, tok], a["xt_lo"][:, j, tok]),
                                 (W.hi[:, j, :], W.lo[:, j, :]), start=j == 0, stop=False)
                    pe.matmul(ps, one[:], bo[:], start=False, stop=True).then_inc(o_ready, 1)

            @block.vector
            def _(v):
                turn.vector(v)
                for t in range(NT):
                    v.wait_ge(o_ready, t + 1)
                    v.scalar_tensor_tensor(X[:, t, :], bank[2 + t % 4][:, 0:D], a["gates"][:, 2:3], X[:, t, :],
                                           ALU.mult, ALU.add).then_inc(o_used, 1)


E = 64
NG = 8
GE = E // NG
TOP = 8
TOP_G = 4
INNER = 176
HALF = INNER // 2
SHARED = 2 * INNER
ITER = 2 * P
STEPS_MAX = T * TOP // ITER + E
SLOTS = STEPS_MAX * ITER
PAR = STEPS_MAX + 2
ZROWS = 4
BIG = 3e38


class Clear:

    def __init__(self, c, slots_d):
        self.Z = c.sb("zero_rows", [P, ZROWS * D])
        self.cleared = c.sem("slots_cleared")
        self.ready = c.sem("zero_rows_ready")
        self.slots_d = slots_d
        self.rows = P * ZROWS
        assert (SLOTS + 2 * ITER) % self.rows == 0
        self.total = (SLOTS + 2 * ITER) // self.rows

    def dma(self, eng, i):
        eng.dma_start(self.slots_d[bass.ds(i * self.rows, self.rows), :].rearrange("(p r) d -> p (r d)", p=P),
                      self.Z[:]).then_inc(self.cleared, 16)

    def wait(self, eng):
        eng.wait_ge(self.cleared, 16 * self.total)


def route_and_share(nc, a, R, slots_d, clear):
    X, XN, bank = a["X"], a["XN"], a["bank"]
    IDX, W8, SH, TBL, BASE = R["IDX"], R["W8"], R["SH"], R["TBL"], R["BASE"]
    with ExitStack() as ctx:
        k = Core(nc, ctx)
        norm = Norm(k, a, "n3")
        GW = Split(k, "gate_w", [P, DC, E], chunks_of(a["w1gate"], D))
        w1 = Split(k, "shared_gu", [P, DC, 2 * SHARED], chunks_of(a["w1sgu"], D))
        w2 = Split(k, "shared_down", [P, 3, D], chunks_of(a["w1sdown"], SHARED))

        def keep(v, t, ps):
            return v.tensor_copy(SH[:, bass.ds(t, 1), :].rearrange("p a d -> p (a d)"), ps)

        ffn = Ffn(k, a, "shared", w1, w2, SHARED, 1.0, keep, low_on_vector=True)
        gbias = k.sb("gate_bias", [P, E])
        tri_g = k.sb("tri_groups", [P, NG * NG])
        tri = k.sb("tri_tokens", [P, P])
        ones = k.sb("ones_full", [P, P])
        steps_of = k.sb("step_numbers", [P, 1])
        SCO = k.sb("scores", [P, NT, E])
        V = k.sb("choice", [P, NT, E])
        A1 = k.sb("route_a", [P, NT, E])
        A2 = k.sb("route_b", [P, NT, E])
        SEL = k.sb("selected", [P, NT, E])
        CUM = k.sb("selected_before", [P, NT + 1, E])
        GS = k.sb("group_score", [P, NT, NG])
        gm = k.sb("group_mask", [P, NT, NG])
        M8 = k.sb("top8", [P, NT, TOP])
        V8 = k.sb("slot8", [P, NT, TOP])
        wsum = k.sb("weight_sum", [P, NT])
        NS = k.sb("expert_steps", [P, E])
        NSI = k.sb("expert_steps_int", [P, E], I32)
        PA = k.sb("prefix_a", [P, 32 + E])
        PBf = k.sb("prefix_b", [P, 32 + E])
        OFF = k.sb("slot_off", [P, E])
        eg = k.sb("expert_of_step", [P, E])
        egc = k.sb("expert_of_step_col", [P, 1])
        ix = [k.sb(f"idx{i}", [P, TOP], U32) for i in range(2)]
        xc = [k.sb(f"xn_row{i}", [P, D]) for i in range(2)]
        loaded = k.sem("r_loaded")
        logits = k.sem("r_logits")
        sco_ready = k.sem("r_sco_ready")
        cum_ready = k.sem("r_cum_ready")
        rank_ready = k.sem("r_rank_ready")
        eg_ready = k.sem("r_eg_ready")
        eg_t = k.sem("r_eg_t")
        idx_ready = k.sem("r_idx_ready")
        copied = k.sem("r_copied")
        scattered = [k.sem(f"r_scattered{i}") for i in range(2)]
        step = k.sem("r_step")
        carrier = k.sem("r_wait_carrier")
        with nc.Block() as block:
            @block.sync
            def _(sp):
                GW.load(sp)
                sp.dma_start(gbias[:], a["gate_bias"].partition_broadcast(P)).then_inc(loaded, 16)
                sp.dma_start(tri_g[:], a["tri_g_d"].partition_broadcast(P)).then_inc(loaded, 16)
                sp.dma_start(tri[:], a["tri_d"]).then_inc(loaded, 16)
                sp.dma_start(steps_of[:], a["step_numbers_d"]).then_inc(loaded, 16)
                w1.load(sp)
                w2.load(sp)

            @block.scalar
            def _(s):
                norm.scalar(s)
                s.wait_ge(logits, 1)
                s.activation(SCO[:], a["banks"][:, 0:2, :].rearrange("p b (t e) -> p (b t) e", e=E),
                             ACT.Sigmoid).then_inc(sco_ready, 1)
                ffn.scalar(s)

            @block.tensor
            def _(pe):
                norm.tensor(pe)
                GW.wait(pe)
                pe.wait_ge(norm.lo_ready, NB * DC)
                for t in range(NT):
                    tok = slice(t * P, (t + 1) * P)
                    for j in range(DC):
                        last = products(pe, bank[t // 8][:, (t % 8) * E:(t % 8 + 1) * E],
                                        (a["xt_hi"][:, j, tok], a["xt_lo"][:, j, tok]),
                                        (GW.hi[:, j, :], GW.lo[:, j, :]), start=j == 0, stop=j == DC - 1)
                last.then_inc(logits, 1)
                pe.wait_ge(cum_ready, NT)
                for h in range(2):
                    tiles = slice(8 * h, 8 * h + 8)
                    pe.matmul(bank[2 + h][:], tri[:], SEL[:, tiles, :].rearrange("p t e -> p (t e)"), start=True, stop=False)
                    pe.matmul(bank[2 + h][:], ones[:], CUM[:, tiles, :].rearrange("p t e -> p (t e)"), start=False, stop=True)
                pe.matmul(bank[4][:, 0:E], ones[:], CUM[:, NT, :], start=True, stop=True).then_inc(rank_ready, 1)
                pe.wait_ge(eg_ready, 1)
                pe.transpose(bank[5][0:1, 0:P], egc[:], a["ident"][:]).then_inc(eg_t, 1)
                pe.wait_ge(idx_ready, 1)
                ffn.tensor(pe, norm)

            @block.gpsimd
            def _(g):
                g.memset(ones[:], 1.0)
                g.memset(PA[:, 0:32], 0.0)
                g.memset(PBf[:, 0:32], 0.0)
                g.memset(CUM[:, 0, :], 0.0)
                g.memset(TBL[:, 0:PAR - 1], E - 1)
                g.memset(TBL[:, PAR - 1:PAR], 0)
                g.memset(TBL[:, PAR:], (E - 1) % 2).then_inc(copied, 1)
                GW.split(g)
                w1.split(g)
                w2.split(g)
                g.wait_ge(idx_ready, 1)
                clear.wait(g)

                def scatter(i, q):
                    g.tensor_copy(ix[q][:], IDX[:, bass.ds(2 * i + q, 1), :].rearrange("p a j -> p (a j)")).then_inc(copied, 1)
                    g.tensor_copy(xc[q][:], XN[:, bass.ds(2 * i + q, 1), :].rearrange("p a j -> p (a j)")).then_inc(copied, 1)
                    g.wait_ge(copied, 1 + 4 * i + 2 * q + 2)
                    g.sem_inc(carrier, 1)
                    for j in range(TOP):
                        g.indirect_dma_start(slots_d, bass.IndirectOffsetOnAxis(ap=ix[q][:, j:j + 1], axis=0),
                                             xc[q][:], None, bounds_check=SLOTS - 1,
                                             oob_is_err=False).then_inc(scattered[q], 16)

                for q in range(2):
                    scatter(0, q)
                with g.Fori(1, NT // 2) as i:
                    for q in range(2):
                        g.wait_ge(scattered[q], 16 * TOP * i)
                        g.sem_inc(carrier, 1)
                        scatter(i, q)
                for q in range(2):
                    g.wait_ge(scattered[q], 16 * TOP * (NT // 2))

            @block.vector
            def _(v):
                norm.vector(v)
                st = Steps(v, step)

                def do(ins):
                    st.inc(ins)
                    st.wait()

                v.wait_ge(copied, 1)
                v.wait_ge(loaded, 64)
                v.wait_ge(sco_ready, 1)
                do(v.tensor_tensor(V[:], SCO[:], gbias[:].unsqueeze(1).to_broadcast([P, NT, E]), ALU.add))
                g4 = V[:].rearrange("p t (g m) -> p (t g) m", m=GE)
                hi1 = A1[:].rearrange("p t e -> p (t e)")[:, 0:512].rearrange("p (g m) -> p g m", m=4)
                lo1 = A1[:].rearrange("p t e -> p (t e)")[:, 512:1024].rearrange("p (g m) -> p g m", m=4)
                f2 = A2[:].rearrange("p t e -> p (t e)")
                hi2, lo2, mn2 = (f2[:, 256 * n:256 * (n + 1)].rearrange("p (g m) -> p g m", m=2) for n in range(3))
                hi3, lo3 = (f2[:, 768 + 128 * n:768 + 128 * (n + 1)].rearrange("p (g m) -> p g m", m=1) for n in range(2))
                st.inc(v.tensor_tensor(hi1, g4[:, :, 0:4], g4[:, :, 4:8], ALU.max))
                do(v.tensor_tensor(lo1, g4[:, :, 0:4], g4[:, :, 4:8], ALU.min))
                st.inc(v.tensor_tensor(hi2, hi1[:, :, 0:2], hi1[:, :, 2:4], ALU.max))
                st.inc(v.tensor_tensor(mn2, hi1[:, :, 0:2], hi1[:, :, 2:4], ALU.min))
                do(v.tensor_tensor(lo2, lo1[:, :, 0:2], lo1[:, :, 2:4], ALU.max))
                do(v.tensor_tensor(lo2, lo2, mn2, ALU.max))
                st.inc(v.tensor_tensor(hi3, hi2[:, :, 0:1], hi2[:, :, 1:2], ALU.max))
                st.inc(v.tensor_tensor(mn2[:, :, 0:1], hi2[:, :, 0:1], hi2[:, :, 1:2], ALU.min))
                do(v.tensor_tensor(lo3, lo2[:, :, 0:1], lo2[:, :, 1:2], ALU.max))
                do(v.tensor_tensor(lo3, lo3, mn2[:, :, 0:1], ALU.max))
                gs = GS[:].rearrange("p t g -> p (t g)").unsqueeze(2)
                do(v.tensor_tensor(gs, hi3, lo3, ALU.add))
                own = GS[:].unsqueeze(3).to_broadcast([P, NT, NG, NG])
                other = GS[:].unsqueeze(2).to_broadcast([P, NT, NG, NG])
                r1 = A1[:].rearrange("p t (g m) -> p t g m", m=NG)
                r2 = A2[:].rearrange("p t (g m) -> p t g m", m=NG)
                st.inc(v.tensor_tensor(r1, other, own, ALU.is_gt))
                do(v.tensor_tensor(r2, other, own, ALU.is_equal))
                do(v.tensor_tensor(A2[:], A2[:], tri_g[:].unsqueeze(1).to_broadcast([P, NT, NG * NG]), ALU.mult))
                do(v.tensor_tensor(A1[:], A1[:], A2[:], ALU.add))
                do(v.tensor_reduce(gm[:], r1, AX_X, ALU.add))
                do(v.tensor_scalar(gm[:], gm[:], float(TOP_G), None, ALU.is_lt))
                do(v.tensor_tensor(A1[:].rearrange("p t (g m) -> p t g m", m=GE),
                                   V[:].rearrange("p t (g m) -> p t g m", m=GE),
                                   gm[:].unsqueeze(3).to_broadcast([P, NT, NG, GE]), ALU.mult))
                do(v.tensor_scalar(A1[:], A1[:], 0.0, None, ALU.add))
                for t in range(NT):
                    st.inc(v.max(M8[:, t, :], A1[:, t, :]))
                st.wait()
                for t in range(NT):
                    st.inc(v.match_replace(A2[:, t, :], M8[:, t, :], A1[:, t, :], -BIG))
                st.wait()
                do(v.tensor_scalar(SEL[:], A2[:], -BIG / 2, None, ALU.is_lt))
                for t in range(NT):
                    v.tensor_tensor(CUM[:, t + 1, :], CUM[:, t, :], SEL[:, t, :], ALU.add).then_inc(cum_ready, 1)
                    v.wait_ge(cum_ready, t + 1)
                do(v.tensor_tensor(SCO[:], SCO[:], SEL[:], ALU.mult))
                do(v.tensor_reduce(wsum[:], SCO[:], AX_X, ALU.add))
                do(v.tensor_scalar(wsum[:], wsum[:], 1e-20, None, ALU.add))
                do(v.reciprocal(wsum[:], wsum[:]))
                do(v.tensor_scalar(wsum[:], wsum[:], 2.5, None, ALU.mult))
                do(v.tensor_tensor(SCO[:], SCO[:], wsum[:].unsqueeze(2).to_broadcast([P, NT, E]), ALU.mult))
                v.wait_ge(rank_ready, 1)
                do(v.tensor_scalar(NSI[:], bank[4][:, 0:E], float(ITER - 1), None, ALU.add))
                do(v.tensor_scalar(NSI[:], NSI[:], 8, None, ALU.logical_shift_right))
                do(v.tensor_scalar(PA[:, 32:], NSI[:], 1.0, None, ALU.max))
                src, dst = PA, PBf
                for d in (1, 2, 4, 8, 16, 32):
                    do(v.tensor_tensor(dst[:, 32:], src[:, 32:], src[:, 32 - d:32 + E - d], ALU.add))
                    src, dst = dst, src
                st.inc(v.tensor_copy(BASE[:], src[0:1, 31:32 + E]))
                do(v.tensor_scalar(eg[:], src[:, 32:], steps_of[:], None, ALU.is_le))
                do(v.tensor_reduce(egc[:], eg[:], AX_X, ALU.add))
                v.tensor_scalar(egc[:], egc[:], float(E - 1), None, ALU.min).then_inc(eg_ready, 1)
                do(v.tensor_scalar(OFF[:], src[:, 31:31 + E], float(-ITER), float(SLOTS), ALU.mult, ALU.add))
                do(v.tensor_tensor(A1[:], OFF[:].unsqueeze(1).to_broadcast([P, NT, E]),
                                   a["banks"][:, 2:4, :].rearrange("p b (t e) -> p (b t) e", e=E), ALU.subtract))
                do(v.tensor_tensor(A1[:], A1[:], SEL[:], ALU.mult))
                for t in range(NT):
                    st.inc(v.max(V8[:, t, :], A1[:, t, :]))
                st.wait()
                do(v.tensor_scalar(IDX[:], V8[:], -1.0, float(SLOTS), ALU.mult, ALU.add))
                do(v.tensor_scalar(R["IDY"][:], V8[:], -1.0, float(SLOTS + ITER), ALU.mult, ALU.add))
                v.wait_ge(eg_t, 1)
                do(v.tensor_copy(TBL[0:1, 0:P], bank[5][0:1, 0:P]))
                v.tensor_scalar(TBL[0:1, PAR:PAR + P], TBL[0:1, 0:P], 1, None, ALU.bitwise_and).then_inc(idx_ready, 1)
                for j in range(TOP):
                    do(v.tensor_tensor(A2[:], A1[:], V8[:, :, j:j + 1].to_broadcast([P, NT, E]), ALU.is_equal))
                    do(v.tensor_tensor(A2[:], A2[:], SCO[:], ALU.mult))
                    do(v.tensor_reduce(W8[:, :, j:j + 1], A2[:], AX_X, ALU.add))
                ffn.vector(v)


def experts(nc, a, R, slots_d, y_d, clear):
    bank, TBL, BASE = a["bank"], R["TBL"], R["BASE"]
    WS = [P, DC, 2 * INNER]
    with ExitStack() as ctx:
        k = Core(nc, ctx)
        raw1, hi1, lo1 = (k.sb(f"e_gu_{n}", [P, 2, DC, 2 * INNER], dt) for n, dt in (("raw", F32), ("hi", F32R), ("lo", F32R)))
        raw2, hi2, lo2 = (k.sb(f"e_down_{n}", [HALF, 2, 2, D], dt) for n, dt in (("raw", F32), ("hi", F32R), ("lo", F32R)))
        XS = k.sb("slot_rows", [P, 2, D])
        XH = k.sb("slot_t_hi", [P, DC, 2, P], F32R)
        XL = k.sb("slot_t_lo", [P, DC, 2, P], F32R)
        SG = k.sb("e_silu", [P, 2, INNER])
        H = k.sb("e_h", [P, 2, INNER])
        HH = k.sb("e_h_hi", [HALF, 2, 2, P], F32R)
        HL = k.sb("e_h_lo", [HALF, 2, 2, P], F32R)
        Y = k.sb("e_y", [P, 2, D])
        raw_loaded = [k.sem(f"e_raw_loaded{i}") for i in range(2)]
        w_hi = k.sem("e_w_hi")
        w_ready = k.sem("e_w_ready")
        x_loaded = k.sem("e_x_loaded")
        x_turned = k.sem("e_x_turned")
        xh_ready = k.sem("e_xh_ready")
        xl_ready = k.sem("e_xl_ready")
        gu_ready = k.sem("e_gu_ready")
        silu_ready = k.sem("e_silu_ready")
        h_ready = k.sem("e_h_ready")
        h_turned = k.sem("e_h_turned")
        hh_ready = k.sem("e_hh_ready")
        hl_ready = k.sem("e_hl_ready")
        y_ps = k.sem("e_y_ps")
        y_ready = k.sem("e_y_ready")
        y_stored = k.sem("e_y_stored")
        carrier = k.sem("e_wait_carrier")
        act_carrier = k.sem("e_act_wait_carrier")
        gate_src = a["w1gu"].rearrange("e (c p) n -> e p c n", p=P)
        down_src = a["w1down"].rearrange("e (c p) n -> e p c n", p=HALF)

        def total(eng):
            return eng.value_load(BASE[0:1, E:E + 1], min_val=E, max_val=STEPS_MAX)

        with nc.Block() as block:
            @block.sync
            def _(sp):
                end = total(sp)
                sp.dma_start(XS[:], slots_d[0:ITER, :].rearrange("(p r) d -> p r d", p=P)).then_inc(x_loaded, 16)
                with sp.Fori(1, end + 2) as s:
                    sp.wait_ge(x_turned, s)
                    sp.dma_start(XS[:], slots_d[bass.ds(s * ITER, ITER), :].rearrange("(p r) d -> p r d", p=P))\
                        .then_inc(x_loaded, 16)
                sp.wait_ge(x_loaded, 16 * (end + 2))
                with sp.Fori(end + 1, STEPS_MAX + 2) as s:
                    sp.dma_start(y_d[bass.ds(s * ITER, ITER), :].rearrange("(p r) d -> p (r d)", p=P),
                                 clear.Z[:, 0:2 * D]).then_inc(x_loaded, 16)
                sp.wait_ge(x_loaded, 16 * (STEPS_MAX + 3))

            @block.gpsimd
            def _(g):
                def load(e, p):
                    g.dma_start(raw1[:, p], gate_src[bass.ds(e, 1)].rearrange("o p c n -> (o p) c n")).then_inc(raw_loaded[p], 16)
                    g.dma_start(raw2[:, p], down_src[bass.ds(e, 1)].rearrange("o p c n -> (o p) c n")).then_inc(raw_loaded[p], 16)

                def split(e, i, p, more):
                    if more:
                        steps = g.value_load(BASE[0:1, bass.ds(e - 1, 1)], min_val=1, max_val=STEPS_MAX)
                        g.wait_ge(y_ps, steps + 1)
                        g.sem_inc(carrier, 1)
                    g.wait_ge(raw_loaded[p], 32 * (i + 1))
                    g.sem_inc(carrier, 1)
                    g.tensor_copy(hi1[:, p], raw1[:, p]).then_inc(w_hi, 1)
                    g.tensor_copy(hi2[:, p], raw2[:, p]).then_inc(w_hi, 1)
                    g.wait_ge(w_hi, 2 * e + 2)
                    g.tensor_tensor(lo1[:, p], raw1[:, p], hi1[:, p].bitcast(F32), ALU.subtract).then_inc(w_ready, 1)
                    g.tensor_tensor(lo2[:, p], raw2[:, p], hi2[:, p].bitcast(F32), ALU.subtract).then_inc(w_ready, 1)
                    g.wait_ge(w_ready, 2 * e + 2)
                    g.sem_inc(carrier, 1)

                load(0, 0)
                load(1, 1)
                for p in range(2):
                    split(p, 0, p, False)
                    load(p + 2, p)
                with g.Fori(1, E // 2 - 1) as i:
                    for p in range(2):
                        split(2 * i + p, i, p, True)
                        load(2 * i + p + 2, p)
                for p in range(2):
                    split(E - 2 + p, E // 2 - 1, p, True)

            @block.tensor
            def _(pe):
                end = total(pe)

                def turn_x(n):
                    pe.wait_ge(x_loaded, 16 * (n + 1))
                    if not (isinstance(n, int) and n == 0):
                        pe.wait_ge(xl_ready, n)
                    for j in range(DC):
                        for q in range(2):
                            last = pe.transpose(bank[0][:, (2 * j + q) * P:(2 * j + q + 1) * P],
                                                XS[:, q, j * P:(j + 1) * P], a["ident"][:])
                    last.then_inc(x_turned, 1)

                turn_x(0)
                with pe.Fori(0, end + 1) as s:
                    e = pe.value_load(TBL[0:1, bass.ds(s, 1)], min_val=0, max_val=E - 1)
                    par = pe.value_load(TBL[0:1, bass.ds(s + PAR, 1)], min_val=0, max_val=1)
                    par_before = pe.value_load(TBL[0:1, bass.ds(s + (PAR - 1), 1)], min_val=0, max_val=1)
                    pe.wait_ge(w_ready, 2 * e + 2)
                    pe.wait_ge(xl_ready, s + 1)
                    pe.wait_ge(h_ready, 2 * s + 2)
                    for q in range(2):
                        for j in range(DC):
                            rhs = tuple(w[:, bass.ds(par, 1), j, :].rearrange("p a n -> p (a n)") for w in (hi1, lo1))
                            last = products(pe, bank[1 + q][:, 0:2 * INNER], (XH[:, j, q, :], XL[:, j, q, :]), rhs,
                                            start=j == 0, stop=j == DC - 1)
                        last.then_inc(gu_ready, 1)
                    turn_x(s + 1)
                    pe.wait_ge(hl_ready, s + 1)
                    pe.wait_ge(y_ready, s + 1)
                    for q in range(2):
                        for j in range(2):
                            rhs = tuple(w[:, bass.ds(par_before, 1), j, :].rearrange("p a n -> p (a n)") for w in (hi2, lo2))
                            last = products(pe, bank[4][:, q * D:(q + 1) * D], (HH[:, j, q, :], HL[:, j, q, :]), rhs,
                                            start=j == 0, stop=j == 1)
                    last.then_inc(y_ps, 1)
                    pe.wait_ge(h_ready, 2 * s + 4)
                    for j in range(2):
                        for q in range(2):
                            last = pe.transpose(bank[3][0:HALF, (2 * j + q) * P:(2 * j + q + 1) * P],
                                                H[:, q, j * HALF:(j + 1) * HALF], a["ident"][:])
                    last.then_inc(h_turned, 1)

            @block.scalar
            def _(s):
                end = total(s)

                def turn_hi(n):
                    s.wait_ge(x_turned, n + 1)
                    if not (isinstance(n, int) and n == 0):
                        s.wait_ge(gu_ready, 2 * n)
                    s.copy(XH[:].rearrange("p c q t -> p (c q t)"), bank[0][:]).then_inc(xh_ready, 1)

                turn_hi(0)
                with s.Fori(0, end + 1) as i:
                    for q in range(2):
                        s.wait_ge(gu_ready, 2 * i + q + 1)
                        s.activation(SG[:, q, :], bank[1 + q][:, 0:INNER], ACT.Silu).then_inc(silu_ready, 1)
                    turn_hi(i + 1)
                    s.wait_ge(y_ps, i + 1)
                    s.wait_ge(y_stored, 16 * i + 16)
                    s.copy(Y[:].rearrange("p q d -> p (q d)"), bank[4][:]).then_inc(y_ready, 1)
                    s.wait_ge(y_ready, i + 2)
                    s.dma_start(y_d[bass.ds(i * ITER, ITER), :].rearrange("(p r) d -> p r d", p=P), Y[:]).then_inc(y_stored, 16)
                    s.wait_ge(h_turned, i + 2)
                    s.copy(HH[:].rearrange("p c q t -> p (c q t)"), bank[3][0:HALF, :]).then_inc(hh_ready, 1)
                s.wait_ge(y_stored, 16 * (end + 2))
                s.sem_inc(act_carrier, 1)

            @block.vector
            def _(v):
                end = total(v)

                def turn_lo(n):
                    v.wait_ge(xh_ready, n + 1)
                    v.tensor_tensor(XL[:].rearrange("p c q t -> p (c q t)"), bank[0][:],
                                    XH[:].rearrange("p c q t -> p (c q t)").bitcast(F32), ALU.subtract).then_inc(xl_ready, 1)

                v.sem_inc(h_ready, 2)
                v.sem_inc(y_ready, 1)
                v.sem_inc(y_stored, 16)
                v.sem_inc(h_turned, 1)
                v.memset(HH[:].bitcast(F32), 0.0).then_inc(hh_ready, 1)
                v.memset(HL[:].bitcast(F32), 0.0).then_inc(hl_ready, 1)
                turn_lo(0)
                with v.Fori(0, end + 1) as i:
                    v.wait_ge(h_turned, i + 1)
                    for q in range(2):
                        v.wait_ge(silu_ready, 2 * i + q + 1)
                        v.tensor_tensor(H[:, q, :], SG[:, q, :], bank[1 + q][:, INNER:2 * INNER],
                                        ALU.mult).then_inc(h_ready, 1)
                    turn_lo(i + 1)
                    v.wait_ge(hh_ready, i + 2)
                    v.tensor_tensor(HL[:].rearrange("p c q t -> p (c q t)"), bank[3][0:HALF, :],
                                    HH[:].rearrange("p c q t -> p (c q t)").bitcast(F32), ALU.subtract).then_inc(hl_ready, 1)


def combine(nc, a, R, y_d):
    X, W8, SH = a["X"], R["W8"], R["SH"]
    with ExitStack() as ctx:
        k = Core(nc, ctx)
        ix = [k.sb(f"idx_y{i}", [P, TOP], U32) for i in range(2)]
        G = [k.sb(f"rows_y{i}", [P, TOP, D]) for i in range(2)]
        copied = k.sem("c_copied")
        gathered = [k.sem(f"c_gathered{i}") for i in range(2)]
        set_ready = k.sem("c_set")
        used = k.sem("c_used")
        step = k.sem("c_step")
        stored = k.sem("c_stored")
        carrier = k.sem("c_wait_carrier")
        with nc.Block() as block:
            @block.gpsimd
            def _(g):
                g.wait_ge(set_ready, 2)
                with g.Fori(0, NT // 2) as i:
                    for q in range(2):
                        g.wait_ge(used, 2 * i + q + 1)
                        g.sem_inc(carrier, 1)
                        g.tensor_copy(ix[q][:], R["IDY"][:, bass.ds(2 * i + q, 1), :].rearrange("p a j -> p (a j)"))\
                            .then_inc(copied, 1)
                        g.wait_ge(copied, 2 * i + q + 1)
                        g.sem_inc(carrier, 1)
                        for j in range(TOP):
                            g.indirect_dma_start(G[q][:, j, :], None, y_d,
                                                 bass.IndirectOffsetOnAxis(ap=ix[q][:, j:j + 1], axis=0),
                                                 bounds_check=SLOTS + ITER - 1, oob_is_err=False).then_inc(gathered[q], 16)

            @block.vector
            def _(v):
                for q in range(2):
                    v.memset(G[q][:], 0.0).then_inc(set_ready, 1)
                v.sem_inc(used, 2)
                with v.Fori(0, NT // 2) as i:
                    for q in range(2):
                        acc = SH[:, bass.ds(2 * i + q, 1), :].rearrange("p a d -> p (a d)")
                        x = X[:, bass.ds(2 * i + q, 1), :].rearrange("p a d -> p (a d)")
                        v.wait_ge(gathered[q], 16 * TOP * (i + 1))
                        for j in range(TOP):
                            v.scalar_tensor_tensor(acc, G[q][:, j, :],
                                                   W8[:, bass.ds(2 * i + q, 1), j:j + 1].rearrange("p a j -> p (a j)"),
                                                   acc, ALU.mult, ALU.add).then_inc(step, 1)
                            v.wait_ge(step, (2 * i + q) * TOP + j + 1)
                        v.scalar_tensor_tensor(x, acc, a["gates"][:, 3:4], x, ALU.mult, ALU.add).then_inc(used, 1)

            @block.sync
            def _(sp):
                out = a["out"].rearrange("a (n p) d -> n p (a d)", p=P)
                with sp.Fori(0, NT) as t:
                    sp.wait_ge(used, t + 3)
                    sp.dma_start(out[bass.ds(t, 1)].rearrange("n p d -> p n d"), X[:, bass.ds(t, 1), :]).then_inc(stored, 16)
                sp.wait_ge(stored, 16 * NT)
def flamingo_two_layers(nc, ins, out):
    with ExitStack() as ctx:
        c = Core(nc, ctx)
        a = dict(ins)
        a["out"] = out
        a["X"] = c.sb("x", [P, NT, D])
        a["XN"] = c.sb("xn", [P, NT, D])
        a["ident"] = c.sb("ident", [P, P])
        a["gates"] = c.sb("gates", [P, 4])
        a["banks"] = ctx.enter_context(nc.psum_tensor("banks", [P, 8, 512], F32))
        a["bank"] = [a["banks"][:, i, :] for i in range(8)]
        a["xt_hi"] = c.sb("xt_hi", [P, DC, T], F32R)
        a["xt_lo"] = c.sb("xt_lo", [P, DC, T], F32R)
        slots_d = nc.dram_tensor("slot_rows_d", (SLOTS + 2 * ITER, D), F32).ap()
        y_d = nc.dram_tensor("expert_rows_d", (SLOTS + 2 * ITER, D), F32).ap()
        clear = Clear(c, slots_d)
        with ExitStack() as ctx0:
            c0 = Core(nc, ctx0)
            w1 = Split(c0, "ffn0_gu", [P, DC, 2 * HIDDEN], chunks_of(a["w0gu"], D), I32)
            w2 = Split(c0, "ffn0_down", [P, HIDDEN // P, D], chunks_of(a["w0down"], HIDDEN), I32)
            l0_attention(nc, a, [w1, w2])
            l0_ffn(nc, a, w1, w2)
        with ExitStack() as ctx1:
            VA = Core(nc, ctx1).sb("values", [P, KT, NH, VW])
            q_d, k_d = ([nc.dram_tensor(f"{n}_{part}", (D, w), F32).ap() for part in ("hi", "lo")]
                        for n, w in (("queries", T), ("keys", SK)))
            l1_projections(nc, a, VA, q_d, k_d)
            l1_attention(nc, a, VA, q_d, k_d, clear)
            l1_output(nc, a)
        R = {"IDX": c.sb("slot_of", [P, NT, TOP], U32), "IDY": c.sb("row_of", [P, NT, TOP], U32),
             "W8": c.sb("weight_of", [P, NT, TOP]), "SH": c.sb("shared_out", [P, NT, D]),
             "TBL": c.sb("step_table", [1, 2 * PAR], I32), "BASE": c.sb("first_step", [1, E + 1], I32)}
        route_and_share(nc, a, R, slots_d, clear)
        experts(nc, a, R, slots_d, y_d, clear)
        combine(nc, a, R, y_d)


def laid_out(inputs):
    import numpy as np
    i = {n: np.asarray(v) for n, v in inputs.items()}
    ctx = i["ctx_1024"][0]
    heads = np.arange(P) // HD
    l0, l1 = "L0_xattn_", "L1_xattn_"
    return {
        "x": i["x"],
        "ctx": ctx,
        "mask": i["mask_Bx1xSxS2_bf0"].reshape(T, S2),
        "gates_d": np.stack([i["g_xattn"][0], i["g_ffn"][0], i["g_xattn"][1], i["g_ffn"][1]]),
        "w0kv": np.concatenate([np.concatenate([i[l0 + "wk_w"].T, i[l0 + "wv_w"].T], 1),
                                np.concatenate([i[l0 + "wk_b"], i[l0 + "wv_b"]])[None]], 0),
        "w0q": i[l0 + "wq_w"],
        "b0q": i[l0 + "wq_b"].reshape(DC, P).T,
        "w0o": i[l0 + "wo_w"].T,
        "b0o": i[l0 + "wo_b"],
        "ln_g": i[l0 + "ln_g"],
        "ln_b": i[l0 + "ln_b"],
        "w0gu": np.concatenate([i["L0_ffn_w_gate"].T, i["L0_ffn_w_up"].T], 1),
        "w0down": i["L0_ffn_w_down"].T,
        "w1qkv": np.concatenate([i[l1 + n].T for n in ("Wq", "Wk", "Wv")], 1),
        "b1qk": np.concatenate([i[l1 + n].reshape(DC, P).T for n in ("bq", "bk")], 1),
        "b1v": i[l1 + "bv"],
        "w1o": i[l1 + "Wo"].T,
        "b1o": i[l1 + "bo"],
        "ctx_t": np.concatenate([ctx, np.repeat(ctx[-1:], SK - S2, 0)]).T,
        "w1gate": i["L1_ffn_gate_w"].T,
        "gate_bias": i["L1_ffn_gate_bias"],
        "w1sgu": np.concatenate([i["L1_ffn_Sg"].T, i["L1_ffn_Su"].T], 1),
        "w1sdown": i["L1_ffn_Sd"].T,
        "w1gu": np.concatenate([i["L1_ffn_Wg"].transpose(0, 2, 1), i["L1_ffn_Wu"].transpose(0, 2, 1)], 2),
        "w1down": i["L1_ffn_Wd"].transpose(0, 2, 1),
        "tri_g_d": np.tril(np.ones((NG, NG), np.float32), -1).reshape(-1),
        "tri_d": np.triu(np.ones((P, P), np.float32), 1),
        "step_numbers_d": np.arange(P, dtype=np.float32)[:, None],
        "ident_d": np.eye(P, dtype=np.float32),
        "head_mask_d": np.where(heads[:, None] == heads[None], 1 / np.sqrt(HD), 0).astype(np.float32),
    }


def kernel(**inputs):
    import numpy as np
    import concourse.bacc as bacc
    from concourse.bass_utils import run_bass_kernel_spmd
    arrays = {n: np.ascontiguousarray(v) for n, v in laid_out(inputs).items()}
    nc = bacc.Bacc("TRN2", target_bir_lowering=False, num_devices=1)
    ins = {n: nc.dram_tensor("in_" + n, v.shape, mybir.dt.from_np(v.dtype), kind="ExternalInput").ap()
           for n, v in arrays.items()}
    out = nc.dram_tensor("out", (1, T, D), F32, kind="ExternalOutput").ap()
    flamingo_two_layers(nc, ins, out)
    r = run_bass_kernel_spmd(nc, [{"in_" + n: v for n, v in arrays.items()}], core_ids=[0])
    return r.results[0]["out"]
```

```python
from contextlib import ExitStack

import concourse.bass as bass
from concourse import mybir

F32 = mybir.dt.float32
F32R = mybir.dt.float32r
I32 = mybir.dt.int32
U8 = mybir.dt.uint8
U32 = mybir.dt.uint32
ACT = mybir.ActivationFunctionType
ALU = mybir.AluOpType
AX_X = mybir.AxisListType.X

P = 128
T = 2048
D = 256
NT = T // P
DC = D // P
S2 = 1601
KT = -(-S2 // P)
SK = KT * P
LAST = S2 - (KT - 1) * P
NH = 16
HD = D // NH
EPS = 1e-5
BLK = 512
NB = T // BLK
HIDDEN = 768


class Steps:

    def __init__(self, eng, sem, base=0):
        self.eng, self.sem, self.base, self.n = eng, sem, base, 0

    def inc(self, ins):
        ins.then_inc(self.sem, 1)
        self.n += 1

    def wait(self):
        self.eng.wait_ge(self.sem, self.base + self.n)


class Core:

    def __init__(self, nc, ctx):
        self.nc, self.ctx, self.sems = nc, ctx, []

    def sb(self, name, shape, dt=F32):
        return self.ctx.enter_context(self.nc.sbuf_tensor(name, shape, dt))

    def sem(self, name):
        self.sems.append(self.ctx.enter_context(self.nc.semaphore(name)))
        return self.sems[-1]


def l0_attention(nc, a, weights):
    X, XN, bank = a["X"], a["XN"], a["bank"]
    ident, gates = a["ident"], a["gates"]
    with ExitStack() as ctx:
        k = Core(nc, ctx)
        C = k.sb("ctx_rows", [P, KT, D + 1])
        WKV = k.sb("w_kv", [P, DC, 2 * D])
        wkv_b = k.sb("w_kv_bias", [1, 2 * D])
        WQ = k.sb("w_q", [P, DC, D])
        BQ = k.sb("b_q", [P, DC])
        WO = k.sb("w_o", [P, DC, D])
        bo = k.sb("b_o", [1, D])
        hm = k.sb("head_mask", [P, P])
        G = k.sb("moments", [P, DC, D + 1])
        g_row = k.sb("moments_row", [1, D + 1])
        T1 = k.sb("moments_k", [P, DC, D])
        t1_row = k.sb("moments_k_row", [1, D])
        M = k.sb("vk", [P, DC, P])
        B = k.sb("vk_o", [P, DC, D])
        A0 = k.sb("q_to_out", [P, DC, D])
        a0_row = k.sb("q_to_out_bias", [1, D])
        lng = k.sb("ln_g", [P, D])
        lnb = k.sb("ln_b", [P, D])
        MSK = k.sb("mask", [P, NT, 401], I32)
        mrow = k.sb("mask_any", [P, NT])
        nan = k.sb("mask_nan", [P, NT])
        one = k.sb("one", [1, P])
        ST = k.sb("ln_stats", [P, NT, 6])
        MV = k.sb("ln_mv", [P, NT, 2])
        var = k.sb("ln_var", [P, NT])
        tmp = k.sb("ln_tmp", [P, NT])
        rt = k.sb("ln_root", [P, NT])
        rs = k.sb("ln_rstd", [P, NT])
        XT = k.sb("xn_t", [P, DC, T])
        Y = XN
        loaded_x = k.sem("l0_loaded_x")
        loaded_c = k.sem("l0_loaded_c")
        loaded_w = k.sem("l0_loaded_w")
        loaded_m = k.sem("l0_loaded_m")
        pad_ready = k.sem("l0_pad_ready")
        ones_ready = k.sem("l0_ones_ready")
        var_ready = k.sem("l0_var_ready")
        sqrt_ready = k.sem("l0_sqrt_ready")
        xn_ready = k.sem("l0_xn_ready")
        xt_ps = k.sem("l0_xt_ps")
        xt_ready = k.sem("l0_xt_ready")
        pe_step = k.sem("l0_pe_step")
        small_copied = k.sem("l0_small_copied")
        m_ready = k.sem("l0_m_ready")
        o_ready = k.sem("l0_o_ready")
        o_used = k.sem("l0_o_used")
        vstep = k.sem("l0_vstep")
        pool_step = k.sem("l0_pool_step")
        with nc.Block() as block:
            @block.sync
            def _(sp):
                sp.dma_start(X[:], a["x"].rearrange("a (n p) d -> p (a n) d", p=P)).then_inc(loaded_x, 16)
                ctx_d = a["ctx"]
                sp.dma_start(C[:, 0:KT - 1, 0:D],
                             ctx_d[0:(KT - 1) * P, :].rearrange("(n p) d -> p n d", p=P)).then_inc(loaded_c, 16)
                sp.dma_start(C[0:LAST, KT - 1, 0:D], ctx_d[(KT - 1) * P:S2, :]).then_inc(loaded_c, 16)
                sp.wait_ge(pad_ready, 1)
                sp.dma_start(MSK[:].bitcast(U8)[:, :, 0:S2],
                             a["mask"].rearrange("(n p) s -> p n s", p=P)).then_inc(loaded_m, 16)
                for w in weights:
                    w.load(sp)

            @block.scalar
            def _(s):
                s.dma_start(ident[:], a["ident_d"]).then_inc(loaded_w, 16)
                s.dma_start(WKV[:], a["w0kv"][0:D, :].rearrange("(c p) n -> p c n", p=P)).then_inc(loaded_w, 16)
                s.dma_start(wkv_b[:], a["w0kv"][D:D + 1, :]).then_inc(loaded_w, 16)
                s.dma_start(WQ[:], a["w0q"].rearrange("(c p) n -> p c n", p=P)).then_inc(loaded_w, 16)
                s.dma_start(BQ[:], a["b0q"]).then_inc(loaded_w, 16)
                s.dma_start(WO[:], a["w0o"].rearrange("(c p) n -> p c n", p=P)).then_inc(loaded_w, 16)
                s.dma_start(bo[:], a["b0o"].rearrange("(o n) -> o n", o=1)).then_inc(loaded_w, 16)
                s.dma_start(hm[:], a["head_mask_d"]).then_inc(loaded_w, 16)
                s.dma_start(lng[:], a["ln_g"].partition_broadcast(P)).then_inc(loaded_w, 16)
                s.dma_start(lnb[:], a["ln_b"].partition_broadcast(P)).then_inc(loaded_w, 16)
                s.dma_start(gates[:], a["gates_d"].partition_broadcast(P)).then_inc(loaded_w, 16)
                s.wait_ge(var_ready, 1)
                s.activation(rt[:], var[:], ACT.Sqrt).then_inc(sqrt_ready, 1)
                s.wait_ge(pe_step, 1)
                for i in range(DC):
                    s.copy(G[:, i, :], bank[i][:, 0:D + 1]).then_inc(small_copied, 1)
                s.copy(g_row[:], bank[2][0:1, 0:D + 1]).then_inc(small_copied, 1)
                s.wait_ge(loaded_w, 11 * 16)
                s.activation(gates[:], gates[:], ACT.Tanh).then_inc(pool_step, 1)
                s.wait_ge(pe_step, 2)
                for i in range(DC):
                    s.copy(T1[:, i, :], bank[3 + i][:, 0:D]).then_inc(small_copied, 1)
                s.copy(t1_row[:], bank[5][0:1, 0:D]).then_inc(small_copied, 1)
                s.wait_ge(pe_step, 4)
                for i in range(DC):
                    s.copy(B[:, i, :], bank[3 + i][:, 0:D]).then_inc(small_copied, 1)
                s.wait_ge(pe_step, 5)
                for i in range(DC):
                    s.copy(A0[:, i, :], bank[i][:, 0:D]).then_inc(small_copied, 1)
                s.copy(a0_row[:], bank[2][0:1, 0:D]).then_inc(small_copied, 1)
                for g in range(NB * DC):
                    s.wait_ge(xt_ps, g + 1)
                    s.copy(XT[:, g % DC, (g // DC) * BLK:(g // DC + 1) * BLK], bank[6 + g % 2][:]).then_inc(xt_ready, 1)
                for w in weights:
                    w.high(s)
                s.wait_ge(var_ready, 2)
                s.activation(rt[:], var[:], ACT.Sqrt).then_inc(sqrt_ready, 1)

            @block.gpsimd
            def _(g):
                g.memset(MSK[:, :, 400:401], 0).then_inc(pad_ready, 1)
                g.memset(C[:, :, D:D + 1], 1.0).then_inc(ones_ready, 1)
                g.memset(one[:], 1.0).then_inc(ones_ready, 1)
                g.wait_ge(loaded_w, 11 * 16)
                g.wait_ge(pool_step, 1)
                g.tensor_scalar(lng[:], lng[:], gates[:, 0:1], None, ALU.mult).then_inc(pool_step, 1)
                g.tensor_scalar(lnb[:], lnb[:], gates[:, 0:1], None, ALU.mult).then_inc(pool_step, 1)
                g.wait_ge(pool_step, 3)
                g.wait_ge(xn_ready, NT)
                for t in range(NT):
                    g.tensor_tensor(X[:, t, :], X[:, t, :], lnb[:], ALU.add).then_inc(pool_step, 1)
                for w in weights:
                    w.low(g)

            @block.tensor
            def _(pe):
                pe.wait_ge(ones_ready, 2)
                pe.wait_ge(loaded_c, 32)
                for s in range(KT):
                    n = P if s < KT - 1 else LAST
                    for i in range(DC + 1):
                        m = P if i < DC else 1
                        last = pe.matmul(bank[i][0:m, 0:D + 1], C[0:n, s, i * P:i * P + m], C[0:n, s, :],
                                         start=s == 0, stop=s == KT - 1)
                last.then_inc(pe_step, 1)
                pe.wait_ge(loaded_w, 11 * 16)
                pe.wait_ge(small_copied, DC + 1)
                for i in range(DC + 1):
                    m = P if i < DC else 1
                    for j in range(DC):
                        pe.matmul(bank[3 + i][0:m, 0:D], G[:, j, i * P:i * P + m], WKV[:, j, 0:D],
                                  start=j == 0, stop=False)
                    last = pe.matmul(bank[3 + i][0:m, 0:D], g_row[:, i * P:i * P + m], wkv_b[:, 0:D],
                                     start=False, stop=True)
                last.then_inc(pe_step, 1)
                pe.wait_ge(small_copied, 2 * (DC + 1))
                for i in range(DC):
                    cols = slice(i * P, (i + 1) * P)
                    vcols = slice(D + i * P, D + (i + 1) * P)
                    for j in range(DC):
                        pe.matmul(bank[i][:, 0:P], WKV[:, j, vcols], T1[:, j, cols], start=j == 0, stop=False)
                    last = pe.matmul(bank[i][:, 0:P], wkv_b[:, vcols], t1_row[:, cols], start=False, stop=True)
                last.then_inc(pe_step, 1)
                pe.wait_ge(m_ready, DC)
                for i in range(DC):
                    last = pe.matmul(bank[3 + i][:, 0:D], M[:, i, :], WO[:, i, :], start=True, stop=True)
                last.then_inc(pe_step, 1)
                pe.wait_ge(small_copied, 2 * (DC + 1) + DC)
                for i in range(DC):
                    for j in range(DC):
                        pe.matmul(bank[i][:, 0:D], WQ[:, j, i * P:(i + 1) * P], B[:, j, :],
                                  start=j == 0, stop=j == DC - 1)
                for j in range(DC):
                    pe.matmul(bank[2][0:1, 0:D], BQ[:, j:j + 1], B[:, j, :], start=j == 0, stop=False)
                pe.matmul(bank[2][0:1, 0:D], one[:, 0:1], bo[:], start=False, stop=True).then_inc(pe_step, 1)
                for g in range(NB * DC):
                    pe.wait_ge(xn_ready, 4 * (g // DC) + 4)
                    if g >= 2:
                        pe.wait_ge(xt_ready, g - 1)
                    for q in range(4):
                        t = 4 * (g // DC) + q
                        last = pe.transpose(bank[6 + g % 2][:, q * P:(q + 1) * P],
                                            XN[:, t, (g % DC) * P:(g % DC + 1) * P], ident[:])
                    last.then_inc(xt_ps, 1)
                pe.wait_ge(small_copied, 3 * (DC + 1) + DC)
                for t in range(NT):
                    pe.wait_ge(xt_ready, DC * (t // 4) + DC)
                    if t >= 4:
                        pe.wait_ge(o_used, t - 3)
                    b = bank[2 + t % 4]
                    for j in range(DC):
                        pe.matmul(b[:, 0:D], XT[:, j, t * P:(t + 1) * P], A0[:, j, :], start=j == 0, stop=False)
                    pe.matmul(b[:, 0:D], one[:], a0_row[:], start=False, stop=True).then_inc(o_ready, 1)

            @block.vector
            def _(v):
                st = Steps(v, vstep)
                v.wait_ge(loaded_x, 16)

                def stats(src):
                    for t in range(NT):
                        st.inc(v.bn_stats(ST[:, t, :], src[:, t, :]))
                    aggregate()

                def aggregate():
                    st.wait()
                    for t in range(NT):
                        st.inc(v.bn_aggr(MV[:, t, :], ST[:, t, :]))
                    st.wait()

                def rstd(n):
                    st.inc(v.tensor_scalar(var[:], MV[:, :, 1], EPS, None, ALU.add))
                    st.wait()
                    v.tensor_copy(tmp[:], var[:]).then_inc(var_ready, 1)
                    v.wait_ge(sqrt_ready, n)
                    v.wait_ge(var_ready, n)
                    dve_newton(v, st, rs, rt, var, tmp)

                stats(X)
                rstd(1)
                for t in range(NT):
                    v.tensor_scalar(XN[:, t, :], X[:, t, :], MV[:, t, 0:1], rs[:, t:t + 1],
                                    ALU.subtract, ALU.mult).then_inc(xn_ready, 1)
                v.wait_ge(pe_step, 3)
                for i in range(DC):
                    v.tensor_tensor(M[:, i, :], bank[i][:, 0:P], hm[:], ALU.mult).then_inc(m_ready, 1)
                v.wait_ge(loaded_m, 16)
                st.inc(v.tensor_reduce(mrow[:], MSK[:], AX_X, ALU.max))
                st.wait()
                st.inc(v.tensor_scalar(nan[:], mrow[:], 0.0, 3e38, ALU.is_gt, ALU.mult))
                st.wait()
                st.inc(v.tensor_scalar(nan[:], nan[:], 10.0, None, ALU.mult))
                st.wait()
                st.inc(v.tensor_tensor(nan[:], nan[:], nan[:], ALU.subtract))
                for t in range(NT):
                    v.wait_ge(o_ready, t + 1)
                    v.tensor_tensor(Y[:, t, :], bank[2 + t % 4][:, 0:D], XN[:, t, :], ALU.add).then_inc(o_used, 1)
                    if t:
                        v.wait_ge(o_used, t)
                        st.inc(v.bn_stats(ST[:, t - 1, :], Y[:, t - 1, :]))
                v.wait_ge(o_used, NT)
                st.inc(v.bn_stats(ST[:, NT - 1, :], Y[:, NT - 1, :]))
                aggregate()
                rstd(2)
                st.inc(v.tensor_tensor(rs[:], rs[:], nan[:], ALU.add))
                st.wait()
                v.wait_ge(pool_step, 3 + NT)
                for t in range(NT):
                    st.inc(v.scalar_tensor_tensor(Y[:, t, :], Y[:, t, :], MV[:, t, 0:1], lng[:], ALU.subtract, ALU.mult))
                st.wait()
                for t in range(NT):
                    st.inc(v.scalar_tensor_tensor(X[:, t, :], Y[:, t, :], rs[:, t:t + 1], X[:, t, :], ALU.mult, ALU.add))
                st.wait()
        return k.sems


def dve_newton(v, st, rs, rt, var, tmp):
    st.inc(v.reciprocal(rs[:], rt[:]))
    st.wait()
    st.inc(v.tensor_tensor(tmp[:], rs[:], rs[:], ALU.mult))
    st.wait()
    st.inc(v.tensor_tensor(tmp[:], tmp[:], var[:], ALU.mult))
    st.wait()
    st.inc(v.tensor_scalar(tmp[:], tmp[:], -0.5, 1.5, ALU.mult, ALU.add))
    st.wait()
    st.inc(v.tensor_tensor(rs[:], rs[:], tmp[:], ALU.mult))
    st.wait()


class Split:

    def __init__(self, c, name, shape, source, dt=F32):
        self.raw = c.sb(name + "_raw", shape, dt)
        self.hi = c.sb(name + "_hi", shape, F32R)
        self.lo = c.sb(name + "_lo", shape, F32R)
        self.dt = dt
        self.loaded = c.sem(name + "_loaded")
        if dt != F32:
            self.cast = c.sem(name + "_cast")
        self.high_ready = c.sem(name + "_high_ready")
        self.ready = c.sem(name + "_split")
        self.source = source
        full = sum(rows == source[0][0] for rows, _ in source)
        self.parts = [(source[0][0], slice(0, full))]
        if full < len(source):
            self.parts.append((source[-1][0], slice(full, full + 1)))

    def load(self, eng):
        self.n = 0
        for j, (rows, src) in enumerate(self.source):
            eng.dma_start(self.raw[0:rows, j, :], src).then_inc(self.loaded, 16)
            self.n += 16

    def high(self, eng):
        eng.wait_ge(self.loaded, 16 * len(self.source))
        copy = eng.copy if isinstance(eng, bass.BassScalarEngine) else eng.tensor_copy
        for n, (rows, chunks) in enumerate(self.parts):
            raw = self.raw[0:rows, chunks, :]
            if self.dt != F32:
                raw = raw.bitcast(F32)
                copy(raw, self.raw[0:rows, chunks, :]).then_inc(self.cast, 1)
                eng.wait_ge(self.cast, n + 1)
            copy(self.hi[0:rows, chunks, :], raw).then_inc(self.high_ready, 1)

    def low(self, eng):
        for n, (rows, chunks) in enumerate(self.parts):
            raw, hi, lo = (m[0:rows, chunks, :] for m in (self.raw, self.hi, self.lo))
            eng.wait_ge(self.high_ready, n + 1)
            eng.tensor_tensor(lo, raw if self.dt == F32 else raw.bitcast(F32), hi.bitcast(F32),
                              ALU.subtract).then_inc(self.ready, 1)

    def split(self, eng):
        self.high(eng)
        self.low(eng)

    def wait(self, eng):
        eng.wait_ge(self.ready, len(self.parts))


def chunks_of(src, rows):
    return [(min(P, rows - r), src[r:min(r + P, rows), :]) for r in range(0, rows, P)]


class Norm:

    def __init__(self, k, a, name):
        self.a = a
        self.ST = k.sb(name + "_stats", [P, NT, 6])
        self.MV = k.sb(name + "_mv", [P, NT, 2])
        self.var = k.sb(name + "_var", [P, NT])
        self.tmp = k.sb(name + "_tmp", [P, NT])
        self.rt = k.sb(name + "_root", [P, NT])
        self.rs = k.sb(name + "_rstd", [P, NT])
        self.step = k.sem(name + "_step")
        self.var_ready = k.sem(name + "_var_ready")
        self.sqrt_ready = k.sem(name + "_sqrt_ready")
        self.xn_ready = k.sem(name + "_xn_ready")
        self.xt_ps = k.sem(name + "_xt_ps")
        self.hi_ready = k.sem(name + "_hi_ready")
        self.lo_ready = k.sem(name + "_lo_ready")

    def statistics(self, v):
        st = Steps(v, self.step)
        for t in range(NT):
            st.inc(v.bn_stats(self.ST[:, t, :], self.a["X"][:, t, :]))
        st.wait()
        for t in range(NT):
            st.inc(v.bn_aggr(self.MV[:, t, :], self.ST[:, t, :]))
        st.wait()
        v.tensor_scalar(self.var[:], self.MV[:, :, 1], EPS, None, ALU.add).then_inc(self.var_ready, 1)

    def normalize(self, v):
        a, st = self.a, Steps(v, self.step, 2 * NT)
        X, XN = a["X"], a["XN"]
        v.wait_ge(self.sqrt_ready, 1)
        dve_newton(v, st, self.rs, self.rt, self.var, self.tmp)
        for t in range(NT):
            v.tensor_scalar(XN[:, t, :], X[:, t, :], self.MV[:, t, 0:1], self.rs[:, t:t + 1],
                            ALU.subtract, ALU.mult).then_inc(self.xn_ready, 1)

    def low(self, v):
        a = self.a
        for g in range(NB * DC):
            b, j = divmod(g, DC)
            v.wait_ge(self.hi_ready, g + 1)
            v.tensor_tensor(a["xt_lo"][:, j, b * BLK:(b + 1) * BLK], a["bank"][6 + g % 2][:],
                            a["xt_hi"][:, j, b * BLK:(b + 1) * BLK].bitcast(F32), ALU.subtract).then_inc(self.lo_ready, 1)

    def root(self, s):
        s.wait_ge(self.var_ready, 1)
        s.activation(self.rt[:], self.var[:], ACT.Sqrt).then_inc(self.sqrt_ready, 1)

    def high(self, s):
        a = self.a
        for g in range(NB * DC):
            b, j = divmod(g, DC)
            s.wait_ge(self.xt_ps, g + 1)
            s.copy(a["xt_hi"][:, j, b * BLK:(b + 1) * BLK], a["bank"][6 + g % 2][:]).then_inc(self.hi_ready, 1)

    def tensor(self, pe):
        a = self.a
        for g in range(NB * DC):
            b, j = divmod(g, DC)
            pe.wait_ge(self.xn_ready, 4 * b + 4)
            if g >= 2:
                pe.wait_ge(self.lo_ready, g - 1)
            for q in range(4):
                last = pe.transpose(a["bank"][6 + g % 2][:, q * P:(q + 1) * P],
                                    a["XN"][:, 4 * b + q, j * P:(j + 1) * P], a["ident"][:])
            last.then_inc(self.xt_ps, 1)


def products(pe, out, lhs, rhs, start, stop):
    (lh, ll), (rh, rl) = lhs, rhs
    pe.matmul(out, lh, rh, start=start, stop=False)
    pe.matmul(out, lh, rl, start=False, stop=False)
    return pe.matmul(out, ll, rh, start=False, stop=stop)


class Ffn:

    def __init__(self, k, a, name, w1, w2, hidden, scale, evacuate, low_on_vector=False):
        self.a, self.w1, self.w2, self.hidden, self.scale, self.evacuate = a, w1, w2, hidden, scale, evacuate
        self.low_on_vector = low_on_vector
        self.sizes = [min(P, hidden - r) for r in range(0, hidden, P)]
        self.n = len(self.sizes)
        self.sg = k.sb(name + "_silu", [P, 2, BLK])
        self.hf = k.sb(name + "_h", [P, 2, BLK])
        self.hh = k.sb(name + "_h_hi", [P, self.n, BLK], F32R)
        self.hl = k.sb(name + "_h_lo", [P, self.n, BLK], F32R)
        self.gu_ready = k.sem(name + "_gu_ready")
        self.silu_ready = k.sem(name + "_silu_ready")
        self.h_ready = k.sem(name + "_h_ready")
        self.hl_ready = k.sem(name + "_hl_ready")
        self.down_done = k.sem(name + "_down_done")
        self.hh_ready = k.sem(name + "_hh_ready")
        self.out_used = k.sem(name + "_out_used")

    def reuse(self, i, c):
        dist = 1 if c == 0 and self.n % 2 else 2
        return i * self.n + c - dist + 3

    def tensor(self, pe, norm):
        a, n = self.a, self.n
        for w in (self.w1, self.w2):
            w.wait(pe)
        with pe.Fori(0, NB) as i:
            pe.wait_ge(norm.lo_ready, i * DC + DC)
            toks = bass.ts(i, BLK)
            for c, m in enumerate(self.sizes):
                pe.wait_ge(self.h_ready, self.reuse(i, c))
                for part in range(2):
                    cols = slice(part * self.hidden + c * P, part * self.hidden + c * P + m)
                    out = a["bank"][2 * (c % 2) + part][0:m, :]
                    for j in range(DC):
                        last = products(pe, out, (self.w1.hi[:, j, cols], self.w1.lo[:, j, cols]),
                                        (a["xt_hi"][:, j, toks], a["xt_lo"][:, j, toks]),
                                        start=j == 0, stop=j == DC - 1)
                last.then_inc(self.gu_ready, 1)
            pe.wait_ge(self.out_used, i * 4 + 4)
            for c, m in enumerate(self.sizes):
                pe.wait_ge(self.hl_ready, i * n + c + 1 + 2)
                for q in range(4):
                    tok = slice(q * P, (q + 1) * P)
                    last = products(pe, a["bank"][4 + q][:, 0:D], (self.hh[0:m, c, tok], self.hl[0:m, c, tok]),
                                    (self.w2.hi[0:m, c, :], self.w2.lo[0:m, c, :]), start=c == 0, stop=c == n - 1)
                last.then_inc(self.down_done, 1)

    def scalar(self, s):
        n = self.n
        with s.Fori(0, NB) as i:
            for c in range(n + 1):
                if c < n:
                    m = self.sizes[c]
                    s.wait_ge(self.gu_ready, i * n + c + 1)
                    s.activation(self.sg[0:m, c % 2, :], self.a["bank"][2 * (c % 2)][0:m, :], ACT.Silu,
                                 scale=self.scale).then_inc(self.silu_ready, 1)
                if c >= 1:
                    m = self.sizes[c - 1]
                    s.wait_ge(self.h_ready, i * n + c + 2)
                    s.wait_ge(self.down_done, i * n + c)
                    s.copy(self.hh[0:m, c - 1, :], self.hf[0:m, (c - 1) % 2, :]).then_inc(self.hh_ready, 1)

    def vector(self, v):
        a, n = self.a, self.n
        v.sem_inc(self.h_ready, 2)
        if self.low_on_vector:
            self.credits(v)
        with v.Fori(0, NB) as i:
            for c in range(n + 1):
                if c < n:
                    m = self.sizes[c]
                    v.wait_ge(self.silu_ready, i * n + c + 1)
                    v.wait_ge(self.hl_ready, self.reuse(i, c))
                    v.tensor_tensor(self.hf[0:m, c % 2, :], self.sg[0:m, c % 2, :],
                                    a["bank"][2 * (c % 2) + 1][0:m, :], ALU.mult).then_inc(self.h_ready, 1)
                if self.low_on_vector and c >= 1:
                    self.low(v, i, c - 1)
            v.wait_ge(self.down_done, i * n + n + n)
            for q in range(4):
                self.evacuate(v, i * 4 + q, a["bank"][4 + q][:, 0:D]).then_inc(self.out_used, 1)

    def credits(self, eng):
        eng.sem_inc(self.hl_ready, 2)
        eng.sem_inc(self.down_done, self.n)
        eng.sem_inc(self.out_used, 4)

    def low(self, eng, i, c):
        m = self.sizes[c]
        eng.wait_ge(self.hh_ready, i * self.n + c + 1)
        eng.tensor_tensor(self.hl[0:m, c, :], self.hf[0:m, c % 2, :], self.hh[0:m, c, :].bitcast(F32),
                          ALU.subtract).then_inc(self.hl_ready, 1)

    def gpsimd(self, g):
        self.credits(g)
        with g.Fori(0, NB) as i:
            for c in range(self.n):
                self.low(g, i, c)


def l0_ffn(nc, a, w1, w2, old_sems):
    with ExitStack() as ctx:
        k = Core(nc, ctx)
        norm = Norm(k, a, "n1")
        coef = k.sb("ffn0_coef", [P, 1])
        coef_ready = k.sem("ffn0_coef_ready")

        def residual(v, t, ps):
            x = a["X"][:, bass.ds(t, 1), :].rearrange("p a d -> p (a d)")
            return v.scalar_tensor_tensor(x, ps, coef[:], x, ALU.mult, ALU.add)

        ffn = Ffn(k, a, "ffn0", w1, w2, HIDDEN, 1 / 127, residual)
        with nc.Block() as block:
            @block.sync
            def _(sp):
                for sem in old_sems:
                    sp.sem_clear(sem)

            @block.tensor
            def _(pe):
                norm.tensor(pe)
                pe.wait_ge(norm.lo_ready, NB * DC)
                ffn.tensor(pe, norm)

            @block.scalar
            def _(s):
                norm.root(s)
                norm.high(s)
                ffn.scalar(s)

            @block.vector
            def _(v):
                norm.statistics(v)
                norm.normalize(v)
                norm.low(v)
                v.wait_ge(coef_ready, 1)
                ffn.vector(v)

            @block.gpsimd
            def _(g):
                g.tensor_scalar(coef[:], a["gates"][:, 1:2], 1 / 127 ** 2, None, ALU.mult).then_inc(coef_ready, 1)
                ffn.gpsimd(g)


class Turn:

    def __init__(self, k, a, name):
        self.a = a
        self.xt_ps = k.sem(name + "_xt_ps")
        self.hi_ready = k.sem(name + "_hi_ready")
        self.lo_ready = k.sem(name + "_lo_ready")

    def vector(self, v):
        a = self.a
        for g in range(NB * DC):
            b, j = divmod(g, DC)
            v.wait_ge(self.hi_ready, g + 1)
            v.tensor_tensor(a["xt_lo"][:, j, b * BLK:(b + 1) * BLK], a["bank"][6 + g % 2][:],
                            a["xt_hi"][:, j, b * BLK:(b + 1) * BLK].bitcast(F32), ALU.subtract).then_inc(self.lo_ready, 1)

    def scalar(self, s):
        a = self.a
        for g in range(NB * DC):
            b, j = divmod(g, DC)
            s.wait_ge(self.xt_ps, g + 1)
            s.copy(a["xt_hi"][:, j, b * BLK:(b + 1) * BLK], a["bank"][6 + g % 2][:]).then_inc(self.hi_ready, 1)

    def tensor(self, pe):
        a = self.a
        for g in range(NB * DC):
            b, j = divmod(g, DC)
            if g >= 2:
                pe.wait_ge(self.lo_ready, g - 1)
            for q in range(4):
                last = pe.transpose(a["bank"][6 + g % 2][:, q * P:(q + 1) * P],
                                    a["XN"][:, 4 * b + q, j * P:(j + 1) * P], a["ident"][:])
            last.then_inc(self.xt_ps, 1)


VW = HD + 1


def l1_projections(nc, a, VA, q_d, k_d, stacks):
    with ExitStack() as ctx:
        k = Core(nc, ctx)
        norm = Norm(k, a, "n2")
        W = Split(k, "l1_w", [P, DC, 3 * D], chunks_of(a["w1qkv"], D))
        CT = Split(k, "ctx_t", [P, DC, SK], chunks_of(a["ctx_t"], D))
        b_qk = k.sb("b_qk", [P, 2 * DC])
        b_v = k.sb("b_v", [1, D])
        one = k.sb("one1", [1, P])
        full = k.sb("qk_full", [P, 2, BLK])
        hi = k.sb("qk_hi", [P, 2, BLK], F32R)
        lo = k.sb("qk_lo", [P, 2, BLK], F32R)
        loaded = k.sem("p1_loaded")
        set_ready = k.sem("p1_set_ready")
        qk_ps = k.sem("p1_qk_ps")
        full_ready = k.sem("p1_full_ready")
        hi_ready = k.sem("p1_hi_ready")
        lo_ready = k.sem("p1_lo_ready")
        hi_out = [k.sem(f"p1_hi_out{i}") for i in range(2)]
        lo_out = [k.sem(f"p1_lo_out{i}") for i in range(2)]
        v_ps = k.sem("p1_v_ps")
        v_ready = k.sem("p1_v_ready")
        pieces = [(D + m * P, CT, n, min(BLK, SK - n), k_d, m) for m in range(DC) for n in range(0, SK, BLK)]
        nk = len(pieces)
        pieces += [(m * P, None, n, BLK, q_d, m) for n in range(0, T, BLK) for m in range(DC)]
        with nc.Block() as block:
            @block.sync
            def _(sp):
                W.load(sp)
                CT.load(sp)
                sp.dma_start(b_qk[:], a["b1qk"]).then_inc(loaded, 16)
                sp.dma_start(b_v[:], a["b1v"].rearrange("(o n) -> o n", o=1)).then_inc(loaded, 16)
                for n, (_, _, c0, w, dram, m) in enumerate(pieces):
                    sp.wait_ge(hi_ready, n + 1)
                    sp.dma_start(dram[0][m * P:(m + 1) * P, c0:c0 + w], hi[:, n % 2, 0:w].bitcast(F32)).then_inc(hi_out[n % 2], 16)
                    sp.wait_ge(lo_ready, n + 1)
                    sp.dma_start(dram[1][m * P:(m + 1) * P, c0:c0 + w], lo[:, n % 2, 0:w].bitcast(F32)).then_inc(lo_out[n % 2], 16)
                for n in range(2):
                    sp.wait_ge(hi_out[n], 8 * len(pieces))
                    sp.wait_ge(lo_out[n], 8 * len(pieces))

            @block.tensor
            def _(pe):
                def piece(n):
                    w0, src, c0, w, _, _ = pieces[n]
                    if n >= 2:
                        pe.wait_ge(full_ready, n - 1)
                    for j in range(DC):
                        rhs = (src.hi[:, j, c0:c0 + w], src.lo[:, j, c0:c0 + w]) if src else \
                            (a["xt_hi"][:, j, c0:c0 + w], a["xt_lo"][:, j, c0:c0 + w])
                        last = products(pe, a["bank"][n % 2][:, 0:w],
                                        (W.hi[:, j, w0:w0 + P], W.lo[:, j, w0:w0 + P]), rhs,
                                        start=j == 0, stop=j == DC - 1)
                    last.then_inc(qk_ps, 1)

                W.wait(pe)
                CT.wait(pe)
                pe.wait_ge(loaded, 32)
                pe.wait_ge(set_ready, 2)
                for n in range(nk):
                    piece(n)
                for s in range(KT):
                    if s >= 4:
                        pe.wait_ge(v_ready, s - 3)
                    b = a["bank"][2 + s % 4][:, 0:D]
                    keys = slice(s * P, (s + 1) * P)
                    for j in range(DC):
                        products(pe, b, (CT.hi[:, j, keys], CT.lo[:, j, keys]),
                                 (W.hi[:, j, 2 * D:3 * D], W.lo[:, j, 2 * D:3 * D]), start=j == 0, stop=False)
                    pe.matmul(b, one[:], b_v[:], start=False, stop=True).then_inc(v_ps, 1)
                norm.tensor(pe)
                pe.wait_ge(norm.lo_ready, NB * DC)
                for n in range(nk, len(pieces)):
                    piece(n)

            @block.scalar
            def _(s):
                W.high(s)
                CT.high(s)
                norm.root(s)
                s.wait_ge(loaded, 32)
                for n, (w0, _, _, w, _, m) in enumerate(pieces):
                    if n == nk:
                        norm.high(s)
                    s.wait_ge(qk_ps, n + 1)
                    if n >= 2:
                        s.wait_ge(lo_ready, n - 1)
                        s.wait_ge(hi_out[n % 2], 16 * (n // 2))
                    bias = b_qk[:, (DC if n < nk else 0) + m:(DC if n < nk else 0) + m + 1]
                    s.activation(full[:, n % 2, 0:w], a["bank"][n % 2][:, 0:w], ACT.Identity,
                                 bias=bias).then_inc(full_ready, 1)
                    s.wait_ge(full_ready, n + 1)
                    s.copy(hi[:, n % 2, 0:w], full[:, n % 2, 0:w]).then_inc(hi_ready, 1)

            @block.gpsimd
            def _(g):
                g.memset(one[:], 1.0).then_inc(set_ready, 1)
                g.memset(VA[:, KT - 1], 0.0).then_inc(set_ready, 1)
                for n, (_, _, _, w, _, _) in enumerate(pieces):
                    g.wait_ge(hi_ready, n + 1)
                    if n >= 2:
                        g.wait_ge(lo_out[n % 2], 16 * (n // 2))
                    g.tensor_tensor(lo[:, n % 2, 0:w], full[:, n % 2, 0:w], hi[:, n % 2, 0:w].bitcast(F32),
                                    ALU.subtract).then_inc(lo_ready, 1)

            @block.vector
            def _(v):
                norm.statistics(v)
                W.low(v)
                CT.low(v)
                norm.normalize(v)
                v.wait_ge(set_ready, 2)
                v.memset(VA[:, 0:KT - 1, :, HD:VW], 1.0)
                v.memset(VA[0:LAST, KT - 1, :, HD:VW], 1.0)
                for s in range(KT):
                    n = P if s < KT - 1 else LAST
                    v.wait_ge(v_ps, s + 1)
                    v.tensor_copy(VA[0:n, s, :, 0:HD],
                                  a["bank"][2 + s % 4][0:n, 0:D].rearrange("p (h d) -> p h d", h=NH)).then_inc(v_ready, 1)
                norm.low(v)
                for qs, ks in stacks:
                    v.memset(qs[:].bitcast(F32), 0.0)
                    v.memset(ks[0:ROW_M, :].bitcast(F32), 0.0)
                    v.memset(ks[ROW_M:P, :].bitcast(F32), 1.0)


NE = NT * 2
KW = 402
SC = NB * KT
SCORE_BANK = [i % 3 if 2 * NB <= i < (KT - 1) * NB else i % 2 for i in range(SC)]


def last_user(i):
    return max(j for j in range(-SC, i) if SCORE_BANK[j % SC] == SCORE_BANK[i])
ROW_M = 96
CLEARS = 3


def l1_attention(nc, a, VA, q_d, k_d, stacks, clear):
    bank, ON = a["bank"], a["XN"]
    with ExitStack() as ctx:
        k = Core(nc, ctx)
        QS, KS = zip(*stacks)
        VH = [k.sb(f"v_head{i}", [P, KT, 32]) for i in range(2)]
        PB = [k.sb(f"probs{i}", [P, T]) for i in range(3)]
        mx = k.sb("row_max2", [P, NT, 2])
        mneg = k.sb("row_max_neg", [P, NT])
        MR = k.sb("max_row", [NT, P], F32R)
        OS = k.sb("out_sum", [P, BLK])
        rec = k.sb("recip", [P, 4, NB, 1])
        stack_loaded = k.sem("a_stack_loaded")
        vh_ready = k.sem("a_vh_ready")
        mx_ready = k.sem("a_mx_ready")
        mx_used = k.sem("a_mx_used")
        mneg_ready = k.sem("a_mneg_ready")
        misc_ready = k.sem("a_misc_ready")
        mr_ready = k.sem("a_mr_ready")
        mrow_loaded = k.sem("a_mrow_loaded")
        score_ready = k.sem("a_score_ready")
        exp_ready = k.sem("a_exp_ready")
        pv_done = k.sem("a_pv_done")
        os_ready = k.sem("a_os_ready")
        on_ready = k.sem("a_on_ready")
        step = k.sem("a_step")
        vh_zero = k.sem("a_vh_zero")

        def load_stack(sp, h, p):
            for dst, (hi_d, lo_d), lo_rows, cols in ((QS[p], q_d, (64,), T), (KS[p], k_d, (32,), SK)):
                for r in (0, 32, 64):
                    src = lo_d if r in lo_rows else hi_d
                    sp.dma_start(dst[r:r + HD, :].bitcast(F32), src[bass.ds(h * HD, HD), :]).then_inc(stack_loaded, 16)

        def put_max(sp, n, p):
            sp.wait_ge(mr_ready, n + 1)
            sp.dma_start(QS[p][ROW_M:ROW_M + 1, :].bitcast(F32).rearrange("o (t q) -> o t q", q=P),
                         MR[:].bitcast(F32)).then_inc(mrow_loaded, 16)

        def sp_window(sp, n, p, following):
            if following:
                sp.wait_ge(exp_ready, SC * n + 2)
                load_stack(sp, n + 1, 1 - p)
                for i in range(CLEARS):
                    clear.dma(sp, CLEARS * n + i + clear.total - CLEARS * (NH - 1))
                put_max(sp, n + 1, 1 - p)

        def pe_max(pe, n, p, e):
            t, half = divmod(e, 2)
            pe.wait_ge(mx_used, n * NE + e + 1)
            for b in range(2):
                key0 = (2 * half + b) * KW
                last = pe.matmul(bank[3 + 2 * (e % 2) + b][:, 0:KW], QS[p][0:ROW_M, t * P:(t + 1) * P],
                                 KS[p][0:ROW_M, key0:key0 + KW], start=True, stop=True)
            last.then_inc(mx_ready, 1)

        def pe_turn_max(pe, n, before):
            pe.wait_ge(mneg_ready, n + 1)
            if before:
                last = max(i for i in range(SC) if SCORE_BANK[i] == 2)
                pe.wait_ge(exp_ready, SC * (n - 1) + last + 3)
            pe.transpose(bank[2][0:NT, 0:P], mneg[:], a["ident"][:]).then_inc(misc_ready, 1)

        def pe_finish(pe, n, following):
            pe.wait_ge(os_ready, n + 1)
            if following:
                pe.wait_ge(mr_ready, n + 2)
            for s in range(4):
                last = pe.transpose(bank[2][:, s * P:(s + 1) * P], OS[:, s * P:(s + 1) * P], a["ident"][:])
            last.then_inc(misc_ready, 1)

        def pe_values(pe, n, p, j):
            pe.wait_ge(exp_ready, SC * n + NB * (j + 1) + 2)
            for qb in range(NB):
                last = pe.matmul(bank[7][32 * qb:32 * qb + 32, :], VH[p][:, j, :],
                                 PB[(j + p) % 3][:, qb * BLK:(qb + 1) * BLK],
                                 start=j == 0, stop=j == KT - 1)
            last.then_inc(pv_done, 1)

        def pe_window(pe, n, p, before, following):
            pe.wait_ge(mrow_loaded, 16 * (n + 1))
            pe.wait_ge(vh_ready, n + 1)
            todo = list(range(NE)) if following else []
            for c in range(KT):
                for qb in range(NB):
                    i = c * NB + qb
                    if i == SCORE_BANK.index(2):
                        pe.wait_ge(on_ready, n + 1)
                    else:
                        pe.wait_ge(exp_ready, SC * n + last_user(i) + 3)
                    pe.matmul(bank[SCORE_BANK[i]][:], KS[p][:, c * P:(c + 1) * P], QS[p][:, qb * BLK:(qb + 1) * BLK],
                              start=True, stop=True).then_inc(score_ready, 1)
                    if c >= 1 and qb % 2 and todo:
                        if c == 1 and qb == 1:
                            pe.wait_ge(stack_loaded, 96 * (n + 2))
                        pe_max(pe, n + 1, 1 - p, todo.pop(0))
                    if c == 0 and qb == 1 and before:
                        pe_finish(pe, n - 1, True)
                    if c == KT - 1 and qb == 1:
                        pe_values(pe, n, p, c - 1)
                        if following:
                            assert not todo
                            pe_turn_max(pe, n + 1, True)
                if 1 <= c < KT - 1:
                    pe_values(pe, n, p, c - 1)
                    if todo:
                        pe_max(pe, n + 1, 1 - p, todo.pop(0))
            pe_values(pe, n, p, KT - 1)

        def act_window(s, n, p):
            for c in range(KT):
                dist = 2 if p == 0 and c < 2 else 3
                s.wait_ge(pv_done, n * KT + c + 1 - dist + 3)
                for qb in range(NB):
                    i = c * NB + qb
                    s.wait_ge(score_ready, SC * n + i + 1)
                    s.activation(PB[(c + p) % 3][:, qb * BLK:(qb + 1) * BLK], bank[SCORE_BANK[i]][:], ACT.Exp,
                                 scale=1 / HD ** 0.5).then_inc(exp_ready, 1)

        def dve_max(v, n, first):
            for e in range(NE):
                v.wait_ge(mx_ready, n * NE + e + 1)
                b = 3 + 2 * (e % 2)
                v.tensor_reduce(mx[:, e // 2, e % 2:e % 2 + 1], a["banks"][:, b:b + 2, 0:KW],
                                mybir.AxisListType.XY, ALU.max).then_inc(mx_used, 1)
            v.wait_ge(mx_used, n * NE + NE + 2)
            v.tensor_reduce(mneg[:], mx[:], AX_X, ALU.max, negate=True).then_inc(mneg_ready, 1)
            v.wait_ge(misc_ready, 1 if first else 2 * n)
            if not first:
                v.wait_ge(mrow_loaded, 16 * n)
            v.tensor_copy(MR[:], bank[2][0:NT, 0:P]).then_inc(mr_ready, 1)

        def dve_finish(v, n, following):
            v.wait_ge(pv_done, (n + 1) * KT + 3)
            v.tensor_copy(OS[:], bank[7][:]).then_inc(os_ready, 1)
            v.wait_ge(misc_ready, 2 * n + (3 if following else 2))
            ps = bank[2][:].rearrange("p (s b r) -> p s b r", s=4, b=NB)
            v.reciprocal(rec[:], ps[:, :, :, HD:VW]).then_inc(step, 1)
            v.wait_ge(step, n + 1)
            v.tensor_tensor(ON[:, :, bass.ds(n * HD, HD)].rearrange("p (b s) d -> p s b d", s=4),
                            ps[:, :, :, 0:HD], rec[:].to_broadcast([P, 4, NB, HD]), ALU.mult).then_inc(on_ready, 1)

        def pool_vh(g, n, p, first):
            if not first:
                g.wait_ge(pv_done, 3 + KT * (n - 1))
                g.sem_inc(a["carrier"], 1)
            g.tensor_copy(VH[p][:, :, 0:VW], VA[:, :, bass.ds(n, 1), :].rearrange("p k o d -> p k (o d)")).then_inc(vh_ready, 1)

        with nc.Block() as block:
            @block.sync
            def _(sp):
                load_stack(sp, 0, 0)
                sp.wait_ge(clear.ready, 1)
                for i in range(clear.total - CLEARS * (NH - 1)):
                    clear.dma(sp, i)
                put_max(sp, 0, 0)
                with sp.Fori(0, NH // 2 - 1) as i:
                    sp_window(sp, 2 * i, 0, True)
                    sp_window(sp, 2 * i + 1, 1, True)
                sp_window(sp, NH - 2, 0, True)
                sp.wait_ge(stack_loaded, 96 * NH)
                sp.wait_ge(mrow_loaded, 16 * NH)

            @block.tensor
            def _(pe):
                pe.wait_ge(stack_loaded, 96)
                for e in range(NE):
                    pe_max(pe, 0, 0, e)
                pe_turn_max(pe, 0, False)
                pe_window(pe, 0, 0, False, True)
                with pe.Fori(0, NH // 2 - 1) as i:
                    pe_window(pe, 2 * i + 1, 1, True, True)
                    pe_window(pe, 2 * i + 2, 0, True, True)
                pe_window(pe, NH - 1, 1, True, False)
                pe_finish(pe, NH - 1, False)

            @block.scalar
            def _(s):
                with s.Fori(0, NH // 2) as i:
                    act_window(s, 2 * i, 0)
                    act_window(s, 2 * i + 1, 1)

            @block.vector
            def _(v):
                v.sem_inc(mx_used, 2)
                v.sem_inc(exp_ready, 2)
                v.sem_inc(pv_done, 3)
                v.sem_inc(on_ready, 1)
                dve_max(v, 0, True)
                dve_max(v, 1, False)
                with v.Fori(1, NH - 1) as n:
                    dve_finish(v, n - 1, True)
                    dve_max(v, n + 1, False)
                dve_finish(v, NH - 2, True)
                dve_finish(v, NH - 1, False)

            @block.gpsimd
            def _(g):
                g.memset(clear.Z[:], 0.0).then_inc(clear.ready, 1)
                for p in range(2):
                    g.memset(VH[p][:], 0.0).then_inc(vh_zero, 1)
                g.wait_ge(vh_zero, 2)
                for p in range(2):
                    pool_vh(g, p, p, True)
                with g.Fori(0, NH // 2 - 1) as i:
                    pool_vh(g, 2 * i + 2, 0, False)
                    pool_vh(g, 2 * i + 3, 1, False)


def l1_output(nc, a):
    X, bank = a["X"], a["bank"]
    with ExitStack() as ctx:
        k = Core(nc, ctx)
        W = Split(k, "l1_wo", [P, DC, D], chunks_of(a["w1o"], D))
        turn = Turn(k, a, "l1_turn")
        bo = k.sb("b1o", [1, D])
        one = k.sb("one2", [1, P])
        loaded = k.sem("o1_loaded")
        one_ready = k.sem("o1_one_ready")
        o_ready = k.sem("o1_ready")
        o_used = k.sem("o1_used")
        with nc.Block() as block:
            @block.sync
            def _(sp):
                W.load(sp)
                sp.dma_start(bo[:], a["b1o"].rearrange("(o n) -> o n", o=1)).then_inc(loaded, 16)

            @block.gpsimd
            def _(g):
                g.memset(one[:], 1.0).then_inc(one_ready, 1)
                W.split(g)

            @block.scalar
            def _(s):
                turn.scalar(s)

            @block.tensor
            def _(pe):
                turn.tensor(pe)
                W.wait(pe)
                pe.wait_ge(loaded, 16)
                pe.wait_ge(one_ready, 1)
                for t in range(NT):
                    pe.wait_ge(turn.lo_ready, DC * (t // 4) + DC)
                    if t >= 4:
                        pe.wait_ge(o_used, t - 3)
                    ps = bank[2 + t % 4][:, 0:D]
                    tok = slice(t * P, (t + 1) * P)
                    for j in range(DC):
                        products(pe, ps, (a["xt_hi"][:, j, tok], a["xt_lo"][:, j, tok]),
                                 (W.hi[:, j, :], W.lo[:, j, :]), start=j == 0, stop=False)
                    pe.matmul(ps, one[:], bo[:], start=False, stop=True).then_inc(o_ready, 1)

            @block.vector
            def _(v):
                turn.vector(v)
                for t in range(NT):
                    v.wait_ge(o_ready, t + 1)
                    v.scalar_tensor_tensor(X[:, t, :], bank[2 + t % 4][:, 0:D], a["gates"][:, 2:3], X[:, t, :],
                                           ALU.mult, ALU.add).then_inc(o_used, 1)


E = 64
NG = 8
GE = E // NG
TOP = 8
TOP_G = 4
INNER = 176
HALF = INNER // 2
SHARED = 2 * INNER
ITER = 2 * P
TILES_MAX = T * TOP // P + E
STEPS_MAX = TILES_MAX // 2
SLOTS = TILES_MAX * P
RING = 8
RAW = 4
AHEAD = RING // 2 - 2
STAGES = 4
ZROWS = 4
BIG = 3e38


class Clear:

    def __init__(self, c, slots_d):
        self.Z = c.sb("zero_rows", [P, ZROWS * D])
        self.cleared = c.sem("slots_cleared")
        self.ready = c.sem("zero_rows_ready")
        self.slots_d = slots_d
        self.rows = P * ZROWS
        self.total = (SLOTS + 3 * ITER + self.rows - 1) // self.rows

    def dma(self, eng, i):
        eng.dma_start(self.slots_d[bass.ds(i * self.rows, self.rows), :].rearrange("(p r) d -> p (r d)", p=P),
                      self.Z[:]).then_inc(self.cleared, 16)

    def wait(self, eng):
        eng.wait_ge(self.cleared, 16 * self.total)


def route_and_share(nc, a, R, slots_d, clear):
    X, XN, bank = a["X"], a["XN"], a["bank"]
    IDX, W8, SH = R["IDX"], R["W8"], R["SH"]
    with ExitStack() as ctx:
        k = Core(nc, ctx)
        norm = Norm(k, a, "n3")
        GW = Split(k, "gate_w", [P, DC, E], chunks_of(a["w1gate"], D))
        w1 = Split(k, "shared_gu", [P, DC, 2 * SHARED], chunks_of(a["w1sgu"], D))
        w2 = Split(k, "shared_down", [P, 3, D], chunks_of(a["w1sdown"], SHARED))

        def keep(v, t, ps):
            return v.tensor_copy(SH[:, bass.ds(t, 1), :].rearrange("p a d -> p (a d)"), ps)

        ffn = Ffn(k, a, "shared", w1, w2, SHARED, 1.0, keep, low_on_vector=True)
        gbias = k.sb("gate_bias", [P, E])
        tri_g = k.sb("tri_groups", [P, NG * NG])
        tri = k.sb("tri_tokens", [P, P])
        ones = k.sb("ones_full", [P, P])
        tiles_of = k.sb("tile_numbers", [P, 2])
        SCO = k.sb("scores", [P, NT, E])
        V = k.sb("choice", [P, NT, E])
        A1 = k.sb("route_a", [P, NT, E])
        A2 = k.sb("route_b", [P, NT, E])
        SEL = k.sb("selected", [P, NT, E])
        CUM = k.sb("selected_before", [P, NT + 1, E])
        GS = k.sb("group_score", [P, NT, NG])
        gm = k.sb("group_mask", [P, NT, NG])
        M8 = k.sb("top8", [P, NT, TOP])
        V8 = k.sb("slot8", [P, NT, TOP])
        wsum = k.sb("weight_sum", [P, NT])
        NSI = k.sb("expert_tiles_int", [P, E], I32)
        PA = k.sb("prefix_a", [P, 32 + E])
        PBf = k.sb("prefix_b", [P, 32 + E])
        OFF = k.sb("slot_off", [P, E])
        eg = k.sb("experts_ended", [P, 2, E])
        egc = k.sb("expert_of_tile_col", [P, 2])
        ix = [k.sb(f"idx{i}", [P, TOP], U32) for i in range(STAGES)]
        xc = [k.sb(f"xn_row{i}", [P, D]) for i in range(STAGES)]
        loaded = k.sem("r_loaded")
        logits = k.sem("r_logits")
        sco_ready = k.sem("r_sco_ready")
        cum_ready = k.sem("r_cum_ready")
        rank_ready = k.sem("r_rank_ready")
        eg_ready = k.sem("r_eg_ready")
        eg_t = k.sem("r_eg_t")
        idx_ready = k.sem("r_idx_ready")
        copied = k.sem("r_copied")
        staged = [k.sem(f"r_staged{i}") for i in range(STAGES)]
        scattered = [k.sem(f"r_scattered{i}") for i in range(STAGES)]
        step = k.sem("r_step")
        with nc.Block() as block:
            @block.sync
            def _(sp):
                GW.load(sp)
                sp.dma_start(gbias[:], a["gate_bias"].partition_broadcast(P)).then_inc(loaded, 16)
                sp.dma_start(tri_g[:], a["tri_g_d"].partition_broadcast(P)).then_inc(loaded, 16)
                sp.dma_start(tri[:], a["tri_d"]).then_inc(loaded, 16)
                sp.dma_start(tiles_of[:], a["tile_numbers_d"]).then_inc(loaded, 16)
                w1.load(sp)
                w2.load(sp)

                def stage(t, q):
                    sp.dma_start(ix[q][:], IDX[:, bass.ds(t, 1), :].rearrange("p a j -> p (a j)")).then_inc(staged[q], 16)
                    sp.dma_start(xc[q][:], XN[:, bass.ds(t, 1), :].rearrange("p a j -> p (a j)")).then_inc(staged[q], 16)

                sp.wait_ge(idx_ready, 1)
                for q in range(STAGES):
                    stage(q, q)
                with sp.Fori(1, NT // STAGES) as i:
                    for q in range(STAGES):
                        sp.wait_ge(scattered[q], 16 * TOP * i)
                        stage(STAGES * i + q, q)

            @block.scalar
            def _(s):
                norm.root(s)
                norm.high(s)
                s.wait_ge(logits, 1)
                s.activation(SCO[:], a["banks"][:, 0:2, :].rearrange("p b (t e) -> p (b t) e", e=E),
                             ACT.Sigmoid).then_inc(sco_ready, 1)
                ffn.scalar(s)

            @block.tensor
            def _(pe):
                norm.tensor(pe)
                GW.wait(pe)
                pe.wait_ge(norm.lo_ready, NB * DC)
                for t in range(NT):
                    tok = slice(t * P, (t + 1) * P)
                    for j in range(DC):
                        last = products(pe, bank[t // 8][:, (t % 8) * E:(t % 8 + 1) * E],
                                        (a["xt_hi"][:, j, tok], a["xt_lo"][:, j, tok]),
                                        (GW.hi[:, j, :], GW.lo[:, j, :]), start=j == 0, stop=j == DC - 1)
                last.then_inc(logits, 1)
                pe.wait_ge(cum_ready, NT)
                for h in range(2):
                    tiles = slice(8 * h, 8 * h + 8)
                    pe.matmul(bank[2 + h][:], tri[:], SEL[:, tiles, :].rearrange("p t e -> p (t e)"), start=True, stop=False)
                    pe.matmul(bank[2 + h][:], ones[:], CUM[:, tiles, :].rearrange("p t e -> p (t e)"), start=False, stop=True)
                pe.matmul(bank[4][:, 0:E], ones[:], CUM[:, NT, :], start=True, stop=True).then_inc(rank_ready, 1)
                pe.wait_ge(eg_ready, 1)
                for h in range(2):
                    last = pe.transpose(bank[5][0:1, h * P:(h + 1) * P], egc[:, h:h + 1], a["ident"][:])
                last.then_inc(eg_t, 1)
                pe.wait_ge(idx_ready, 1)
                ffn.tensor(pe, norm)

            @block.gpsimd
            def _(g):
                g.memset(ones[:], 1.0)
                g.memset(PA[:, 0:32], 0.0)
                g.memset(PBf[:, 0:32], 0.0)
                g.memset(CUM[:, 0, :], 0.0)
                g.memset(R["RING_OF"][:, 0:2], 0).then_inc(copied, 1)
                GW.split(g)
                w1.split(g)
                w2.split(g)
                g.wait_ge(idx_ready, 1)
                clear.wait(g)

                with g.Fori(0, NT // STAGES) as i:
                    for q in range(STAGES):
                        g.wait_ge(staged[q], 32 * i + 32)
                        g.sem_inc(a["carrier"], 1)
                        for j in range(TOP):
                            g.indirect_dma_start(slots_d, bass.IndirectOffsetOnAxis(ap=ix[q][:, j:j + 1], axis=0),
                                                 xc[q][:], None, bounds_check=SLOTS - 1,
                                                 oob_is_err=False).then_inc(scattered[q], 16)
                for q in range(STAGES):
                    g.wait_ge(scattered[q], 16 * TOP * (NT // STAGES))

            @block.vector
            def _(v):
                norm.statistics(v)
                norm.normalize(v)
                norm.low(v)
                st = Steps(v, step)

                def do(ins):
                    st.inc(ins)
                    st.wait()

                v.wait_ge(copied, 1)
                v.wait_ge(loaded, 64)
                v.wait_ge(sco_ready, 1)
                do(v.tensor_tensor(V[:], SCO[:], gbias[:].unsqueeze(1).to_broadcast([P, NT, E]), ALU.add))
                g4 = V[:].rearrange("p t (g m) -> p (t g) m", m=GE)
                hi1 = A1[:].rearrange("p t e -> p (t e)")[:, 0:512].rearrange("p (g m) -> p g m", m=4)
                lo1 = A1[:].rearrange("p t e -> p (t e)")[:, 512:1024].rearrange("p (g m) -> p g m", m=4)
                f2 = A2[:].rearrange("p t e -> p (t e)")
                hi2, lo2, mn2 = (f2[:, 256 * n:256 * (n + 1)].rearrange("p (g m) -> p g m", m=2) for n in range(3))
                hi3, lo3 = (f2[:, 768 + 128 * n:768 + 128 * (n + 1)].rearrange("p (g m) -> p g m", m=1) for n in range(2))
                st.inc(v.tensor_tensor(hi1, g4[:, :, 0:4], g4[:, :, 4:8], ALU.max))
                do(v.tensor_tensor(lo1, g4[:, :, 0:4], g4[:, :, 4:8], ALU.min))
                st.inc(v.tensor_tensor(hi2, hi1[:, :, 0:2], hi1[:, :, 2:4], ALU.max))
                st.inc(v.tensor_tensor(mn2, hi1[:, :, 0:2], hi1[:, :, 2:4], ALU.min))
                do(v.tensor_tensor(lo2, lo1[:, :, 0:2], lo1[:, :, 2:4], ALU.max))
                do(v.tensor_tensor(lo2, lo2, mn2, ALU.max))
                st.inc(v.tensor_tensor(hi3, hi2[:, :, 0:1], hi2[:, :, 1:2], ALU.max))
                st.inc(v.tensor_tensor(mn2[:, :, 0:1], hi2[:, :, 0:1], hi2[:, :, 1:2], ALU.min))
                do(v.tensor_tensor(lo3, lo2[:, :, 0:1], lo2[:, :, 1:2], ALU.max))
                do(v.tensor_tensor(lo3, lo3, mn2[:, :, 0:1], ALU.max))
                gs = GS[:].rearrange("p t g -> p (t g)").unsqueeze(2)
                do(v.tensor_tensor(gs, hi3, lo3, ALU.add))
                own = GS[:].unsqueeze(3).to_broadcast([P, NT, NG, NG])
                other = GS[:].unsqueeze(2).to_broadcast([P, NT, NG, NG])
                r1 = A1[:].rearrange("p t (g m) -> p t g m", m=NG)
                r2 = A2[:].rearrange("p t (g m) -> p t g m", m=NG)
                st.inc(v.tensor_tensor(r1, other, own, ALU.is_gt))
                do(v.tensor_tensor(r2, other, own, ALU.is_equal))
                do(v.tensor_tensor(A2[:], A2[:], tri_g[:].unsqueeze(1).to_broadcast([P, NT, NG * NG]), ALU.mult))
                do(v.tensor_tensor(A1[:], A1[:], A2[:], ALU.add))
                do(v.tensor_reduce(gm[:], r1, AX_X, ALU.add))
                do(v.tensor_scalar(gm[:], gm[:], float(TOP_G), None, ALU.is_lt))
                do(v.tensor_tensor(A1[:].rearrange("p t (g m) -> p t g m", m=GE),
                                   V[:].rearrange("p t (g m) -> p t g m", m=GE),
                                   gm[:].unsqueeze(3).to_broadcast([P, NT, NG, GE]), ALU.mult))
                do(v.tensor_scalar(A1[:], A1[:], 0.0, None, ALU.add))
                for t in range(NT):
                    st.inc(v.max(M8[:, t, :], A1[:, t, :]))
                st.wait()
                for t in range(NT):
                    st.inc(v.match_replace(A2[:, t, :], M8[:, t, :], A1[:, t, :], -BIG))
                st.wait()
                do(v.tensor_scalar(SEL[:], A2[:], -BIG / 2, None, ALU.is_lt))
                for t in range(NT):
                    v.tensor_tensor(CUM[:, t + 1, :], CUM[:, t, :], SEL[:, t, :], ALU.add).then_inc(cum_ready, 1)
                    v.wait_ge(cum_ready, t + 1)
                do(v.tensor_tensor(SCO[:], SCO[:], SEL[:], ALU.mult))
                do(v.tensor_reduce(wsum[:], SCO[:], AX_X, ALU.add))
                do(v.tensor_scalar(wsum[:], wsum[:], 1e-20, None, ALU.add))
                do(v.reciprocal(wsum[:], wsum[:]))
                do(v.tensor_scalar(wsum[:], wsum[:], 2.5, None, ALU.mult))
                do(v.tensor_tensor(SCO[:], SCO[:], wsum[:].unsqueeze(2).to_broadcast([P, NT, E]), ALU.mult))
                v.wait_ge(rank_ready, 1)
                do(v.tensor_scalar(NSI[:], bank[4][:, 0:E], float(P - 1), None, ALU.add))
                do(v.tensor_scalar(NSI[:], NSI[:], P.bit_length() - 1, None, ALU.logical_shift_right))
                do(v.tensor_scalar(PA[:, 32:], NSI[:], 1.0, None, ALU.max))
                src, dst = PA, PBf
                for d in (1, 2, 4, 8, 16, 32):
                    do(v.tensor_tensor(dst[:, 32:], src[:, 32:], src[:, 32 - d:32 + E - d], ALU.add))
                    src, dst = dst, src
                for h in range(2):
                    st.inc(v.tensor_scalar(eg[:, h, :], src[:, 32:], tiles_of[:, h:h + 1], None, ALU.is_le))
                st.wait()
                do(v.tensor_reduce(egc[:], eg[:], AX_X, ALU.add))
                v.tensor_scalar(egc[:], egc[:], float(E - 1), None, ALU.min).then_inc(eg_ready, 1)
                do(v.tensor_scalar(R["STEPS"][:], src[0:1, 31 + E:32 + E], 1.0, None, ALU.add))
                do(v.tensor_scalar(R["STEPS"][:], R["STEPS"][:], 1, None, ALU.logical_shift_right))
                do(v.tensor_scalar(OFF[:], src[:, 31:31 + E], float(-P), float(SLOTS), ALU.mult, ALU.add))
                do(v.tensor_tensor(A1[:], OFF[:].unsqueeze(1).to_broadcast([P, NT, E]),
                                   a["banks"][:, 2:4, :].rearrange("p b (t e) -> p (b t) e", e=E), ALU.subtract))
                do(v.tensor_tensor(A1[:], A1[:], SEL[:], ALU.mult))
                for t in range(NT):
                    st.inc(v.max(V8[:, t, :], A1[:, t, :]))
                st.wait()
                do(v.tensor_scalar(IDX[:], V8[:], -1.0, float(SLOTS), ALU.mult, ALU.add))
                do(v.tensor_scalar(R["IDY"][:], V8[:], -1.0, float(SLOTS + ITER), ALU.mult, ALU.add))
                v.wait_ge(eg_t, 1)
                eot, ring_of, word, span = (R[n] for n in ("EXPERT_OF", "RING_OF", "WORD", "SPAN"))
                do(v.tensor_copy(eot[:], bank[5][0:1, 0:2 * P]))
                do(v.tensor_scalar(ring_of[:, 2:], eot[:], RING - 1, None, ALU.bitwise_and))
                places = ring_of[:].rearrange("o (s q) -> o s q", q=2)
                experts = eot[:].rearrange("o (s q) -> o s q", q=2)
                do(v.scalar_tensor_tensor(word[:], experts[:, :, 1], float(RING), places[:, 0:P, 1], ALU.mult, ALU.add))
                for part in (places[:, 0:P, 0], places[:, 1:P + 1, 1], places[:, 1:P + 1, 0]):
                    do(v.scalar_tensor_tensor(word[:], word[:], float(RING), part, ALU.mult, ALU.add))
                n = STEPS_MAX + 1
                v.scalar_tensor_tensor(span[:, 0:n], experts[:, AHEAD:AHEAD + n, 1], float(E),
                                       experts[:, AHEAD - 1:AHEAD - 1 + n, 1], ALU.mult, ALU.add).then_inc(idx_ready, 1)
                for j in range(TOP):
                    do(v.tensor_tensor(A2[:], A1[:], V8[:, :, j:j + 1].to_broadcast([P, NT, E]), ALU.is_equal))
                    do(v.tensor_tensor(A2[:], A2[:], SCO[:], ALU.mult))
                    do(v.tensor_reduce(W8[:, :, j:j + 1], A2[:], AX_X, ALU.add))
                ffn.vector(v)


def experts(nc, a, R, slots_d, y_d, clear):
    bank = a["bank"]
    EXPERT_OF, WORD, SPAN, STEPS = (R[n] for n in ("EXPERT_OF", "WORD", "SPAN", "STEPS"))
    with ExitStack() as ctx:
        k = Core(nc, ctx)
        raw1 = k.sb("e_gu_raw", [P, RAW, DC, 2 * INNER])
        raw2 = k.sb("e_down_raw", [HALF, RAW, 2, D])
        hi1, lo1 = (k.sb(f"e_gu_{n}", [P, RING, DC, 2 * INNER], F32R) for n in ("hi", "lo"))
        hi2, lo2 = (k.sb(f"e_down_{n}", [HALF, RING, 2, D], F32R) for n in ("hi", "lo"))
        XS = k.sb("slot_rows", [P, 2, D])
        XH = k.sb("slot_t_hi", [P, DC, 2, P], F32R)
        XL = k.sb("slot_t_lo", [P, DC, 2, P], F32R)
        SG = k.sb("e_silu", [P, 2, INNER])
        H = k.sb("e_h", [P, 2, INNER])
        HH = k.sb("e_h_hi", [HALF, 2, 2, P], F32R)
        HL = k.sb("e_h_lo", [HALF, 2, 2, P], F32R)
        Y = k.sb("e_y", [P, 2, D])
        raw_loaded = [k.sem(f"e_raw_loaded{i}") for i in range(RAW)]
        raw_here = k.sem("e_raw_here")
        w_hi = k.sem("e_w_hi")
        w_ready = k.sem("e_w_ready")
        x_loaded = k.sem("e_x_loaded")
        x_turned = k.sem("e_x_turned")
        xh_ready = k.sem("e_xh_ready")
        xl_ready = k.sem("e_xl_ready")
        gu_ready = k.sem("e_gu_ready")
        silu_ready = k.sem("e_silu_ready")
        h_ready = k.sem("e_h_ready")
        h_turned = k.sem("e_h_turned")
        hh_ready = k.sem("e_hh_ready")
        hl_ready = k.sem("e_hl_ready")
        y_ps = k.sem("e_y_ps")
        y_ready = k.sem("e_y_ready")
        y_stored = k.sem("e_y_stored")
        y_cleared = k.sem("e_y_cleared")
        gate_src = a["w1gu"].rearrange("e (c p) n -> e p c n", p=P)
        down_src = a["w1down"].rearrange("e (c p) n -> e p c n", p=HALF)

        def total(eng):
            return eng.value_load(STEPS[0:1, 0:1], min_val=E // 2, max_val=STEPS_MAX)

        def rows(dram, s):
            return dram[bass.ds(s * ITER, ITER), :].rearrange("(r p) d -> p r d", p=P)

        with nc.Block() as block:
            @block.sync
            def _(sp):
                def load(e, p):
                    sp.dma_start(raw1[:, p], gate_src[bass.ds(e, 1)].rearrange("o p c n -> (o p) c n")).then_inc(raw_loaded[p], 16)
                    sp.dma_start(raw2[:, p], down_src[bass.ds(e, 1)].rearrange("o p c n -> (o p) c n")).then_inc(raw_loaded[p], 16)

                def arrived(e, i, p):
                    sp.wait_ge(raw_loaded[p], 32 * (i + 1))
                    sp.sem_inc(raw_here, 1)

                def load_ahead(e, p):
                    sp.wait_ge(w_ready, 2 * e)
                    load(e + RAW - 1, (p + RAW - 1) % RAW)

                for p in range(RAW):
                    load(p, p)
                arrived(0, 0, 0)
                for p in range(1, RAW):
                    arrived(p, 0, p)
                    load_ahead(p, p)
                with sp.Fori(1, E // RAW - 1) as i:
                    for p in range(RAW):
                        arrived(RAW * i + p, i, p)
                        load_ahead(RAW * i + p, p)
                for p in range(RAW):
                    arrived(E - RAW + p, E // RAW - 1, p)
                    if p == 0:
                        load_ahead(E - RAW, 0)
                end = total(sp)
                with sp.Fori(end + 1, STEPS_MAX + 2) as s:
                    sp.dma_start(y_d[bass.ds(s * ITER, ITER), :].rearrange("(p r) d -> p (r d)", p=P),
                                 clear.Z[:, 0:2 * D]).then_inc(y_cleared, 16)
                sp.wait_ge(y_cleared, 16 * (STEPS_MAX + 2))

            @block.gpsimd
            def _(g):
                with g.Fori(0, E // RING) as i:
                    for p in range(RING):
                        g.wait_ge(w_hi, 2 * (RING * i + p) + 2)
                        g.sem_inc(a["carrier"], 1)
                        g.tensor_tensor(lo1[:, p], raw1[:, p % RAW], hi1[:, p].bitcast(F32), ALU.subtract).then_inc(w_ready, 1)
                        g.tensor_tensor(lo2[:, p], raw2[:, p % RAW], hi2[:, p].bitcast(F32), ALU.subtract).then_inc(w_ready, 1)

            @block.tensor
            def _(pe):
                end = total(pe)

                def turn_x(n):
                    pe.wait_ge(x_loaded, 16 * (n + 1))
                    for j in range(DC):
                        for q in range(2):
                            last = pe.transpose(bank[0][:, (2 * j + q) * P:(2 * j + q + 1) * P],
                                                XS[:, q, j * P:(j + 1) * P], a["ident"][:])
                    last.then_inc(x_turned, 1)

                turn_x(0)
                with pe.Fori(0, end + 1) as s:
                    pe.wait_ge(h_ready, 2 * s + 2)
                    for j in range(2):
                        for q in range(2):
                            last = pe.transpose(bank[3][0:HALF, (2 * j + q) * P:(2 * j + q + 1) * P],
                                                H[:, q, j * HALF:(j + 1) * HALF], a["ident"][:])
                    last.then_inc(h_turned, 1)
                    word = pe.value_load(WORD[0:1, bass.ds(s, 1)], min_val=0, max_val=RING ** 4 * E - 1)
                    now = [word % RING, word // RING % RING]
                    before = [word // RING ** 2 % RING, word // RING ** 3 % RING]
                    e = word // RING ** 4
                    pe.wait_ge(xl_ready, s + 1)
                    turn_x(s + 1)
                    pe.wait_ge(w_ready, 2 * e + 2)
                    for q in range(2):
                        for j in range(DC):
                            rhs = tuple(w[:, bass.ds(now[q], 1), j, :].rearrange("p a n -> p (a n)") for w in (hi1, lo1))
                            last = products(pe, bank[1 + q][:, 0:2 * INNER], (XH[:, j, q, :], XL[:, j, q, :]), rhs,
                                            start=j == 0, stop=j == DC - 1)
                        last.then_inc(gu_ready, 1)
                    pe.wait_ge(hl_ready, s + 1)
                    pe.wait_ge(y_ready, s + 1)
                    for q in range(2):
                        for j in range(2):
                            rhs = tuple(w[:, bass.ds(before[q], 1), j, :].rearrange("p a n -> p (a n)") for w in (hi2, lo2))
                            last = products(pe, bank[4][:, q * D:(q + 1) * D], (HH[:, j, q, :], HL[:, j, q, :]), rhs,
                                            start=j == 0, stop=j == 1)
                    last.then_inc(y_ps, 1)

            @block.scalar
            def _(s):
                end = total(s)

                def load_x(n):
                    s.dma_start(XS[:], rows(slots_d, n)).then_inc(x_loaded, 16)

                def turn_hi(n):
                    s.copy(XH[:].rearrange("p c q t -> p (c q t)"), bank[0][:]).then_inc(xh_ready, 1)

                load_x(0)
                s.wait_ge(x_turned, 1)
                load_x(1)
                turn_hi(0)
                with s.Fori(0, end + 1) as i:
                    s.wait_ge(h_turned, i + 1)
                    s.copy(HH[:].rearrange("p c q t -> p (c q t)"), bank[3][0:HALF, :]).then_inc(hh_ready, 1)
                    s.wait_ge(x_turned, i + 2)
                    load_x(i + 2)
                    for q in range(2):
                        s.wait_ge(gu_ready, 2 * i + q + 1)
                        s.activation(SG[:, q, :], bank[1 + q][:, 0:INNER], ACT.Silu).then_inc(silu_ready, 1)
                    turn_hi(i + 1)
                    s.wait_ge(y_ps, i + 3)
                    s.wait_ge(y_stored, 16 * i + 16)
                    s.copy(Y[:].rearrange("p q d -> p (q d)"), bank[4][:]).then_inc(y_ready, 1)
                    s.wait_ge(y_ready, i + 2)
                    s.dma_start(rows(y_d, i), Y[:]).then_inc(y_stored, 16)
                    s.sem_inc(y_cleared, 16)
                s.wait_ge(y_stored, 16 * (end + 2))
                s.wait_ge(x_loaded, 16 * (end + 3))
                s.sem_inc(a["carrier"], 1)

            @block.vector
            def _(v):
                end = total(v)

                def turn_lo(n):
                    v.wait_ge(xh_ready, n + 1)
                    v.tensor_tensor(XL[:].rearrange("p c q t -> p (c q t)"), bank[0][:],
                                    XH[:].rearrange("p c q t -> p (c q t)").bitcast(F32), ALU.subtract).then_inc(xl_ready, 1)

                def high_parts(first, past):
                    with v.If(past > first):
                        with v.Fori(first, past) as e:
                            place, raw = e % RING, e % RAW
                            v.wait_ge(raw_here, e + 1)
                            v.tensor_copy(hi1[:, bass.ds(place, 1)], raw1[:, bass.ds(raw, 1)]).then_inc(w_hi, 1)
                            v.tensor_copy(hi2[:, bass.ds(place, 1)], raw2[:, bass.ds(raw, 1)]).then_inc(w_hi, 1)

                v.sem_inc(y_ready, 1)
                v.sem_inc(y_stored, 16)
                v.sem_inc(y_ps, 2)
                v.memset(H[:], 0.0).then_inc(h_ready, 2)
                turn_lo(0)
                last = v.value_load(EXPERT_OF[0:1, 2 * AHEAD - 1:2 * AHEAD], min_val=0, max_val=E - 1)
                high_parts(0 * end, last + 1)
                with v.Fori(0, end + 1) as i:
                    v.wait_ge(hh_ready, i + 1)
                    v.tensor_tensor(HL[:].rearrange("p c q t -> p (c q t)"), bank[3][0:HALF, :],
                                    HH[:].rearrange("p c q t -> p (c q t)").bitcast(F32), ALU.subtract).then_inc(hl_ready, 1)
                    for q in range(2):
                        v.wait_ge(silu_ready, 2 * i + q + 1)
                        v.tensor_tensor(H[:, q, :], SG[:, q, :], bank[1 + q][:, INNER:2 * INNER],
                                        ALU.mult).then_inc(h_ready, 1)
                    turn_lo(i + 1)
                    v.wait_ge(y_ps, i + 2)
                    span = v.value_load(SPAN[0:1, bass.ds(i, 1)], min_val=0, max_val=E * E - 1)
                    high_parts(span % E + 1, span // E + 1)


def combine(nc, a, R, y_d):
    X, W8, SH = a["X"], R["W8"], R["SH"]
    with ExitStack() as ctx:
        k = Core(nc, ctx)
        ix = [k.sb(f"idx_y{i}", [P, TOP], U32) for i in range(STAGES)]
        G = [k.sb(f"rows_y{i}", [P, TOP, D]) for i in range(STAGES)]
        staged = [k.sem(f"c_staged{i}") for i in range(STAGES)]
        gathered = [k.sem(f"c_gathered{i}") for i in range(STAGES)]
        set_ready = k.sem("c_set")
        used = k.sem("c_used")
        step = k.sem("c_step")
        stored = k.sem("c_stored")
        with nc.Block() as block:
            @block.gpsimd
            def _(g):
                g.wait_ge(set_ready, STAGES)
                with g.Fori(0, NT // STAGES) as i:
                    for q in range(STAGES):
                        g.wait_ge(used, STAGES * i + q + 1)
                        g.sem_inc(a["carrier"], 1)
                        g.wait_ge(staged[q], 16 * i + 16)
                        g.sem_inc(a["carrier"], 1)
                        for j in range(TOP):
                            g.indirect_dma_start(G[q][:, j, :], None, y_d,
                                                 bass.IndirectOffsetOnAxis(ap=ix[q][:, j:j + 1], axis=0),
                                                 bounds_check=SLOTS + ITER - 1, oob_is_err=False).then_inc(gathered[q], 16)

            @block.vector
            def _(v):
                v.sem_inc(used, STAGES)
                for q in range(STAGES):
                    v.memset(G[q][:], 0.0).then_inc(set_ready, 1)
                with v.Fori(0, NT // STAGES) as i:
                    for q in range(STAGES):
                        acc = SH[:, bass.ds(STAGES * i + q, 1), :].rearrange("p a d -> p (a d)")
                        x = X[:, bass.ds(STAGES * i + q, 1), :].rearrange("p a d -> p (a d)")
                        v.wait_ge(gathered[q], 16 * TOP * (i + 1))
                        for j in range(TOP):
                            v.scalar_tensor_tensor(acc, G[q][:, j, :],
                                                   W8[:, bass.ds(STAGES * i + q, 1), j:j + 1].rearrange("p a j -> p (a j)"),
                                                   acc, ALU.mult, ALU.add).then_inc(step, 1)
                            v.wait_ge(step, (STAGES * i + q) * TOP + j + 1)
                        v.scalar_tensor_tensor(x, acc, a["gates"][:, 3:4], x, ALU.mult, ALU.add).then_inc(used, 1)

            @block.sync
            def _(sp):
                out = a["out"].rearrange("a (n p) d -> n p (a d)", p=P)

                def stage(t, q):
                    sp.dma_start(ix[q][:], R["IDY"][:, bass.ds(t, 1), :].rearrange("p a j -> p (a j)")).then_inc(staged[q], 16)

                for q in range(STAGES):
                    stage(q, q)
                with sp.Fori(0, NT // STAGES - 1) as i:
                    for q in range(STAGES):
                        t = STAGES * i + q
                        sp.wait_ge(used, t + STAGES + 1)
                        stage(t + STAGES, q)
                        sp.dma_start(out[bass.ds(t, 1)].rearrange("n p d -> p n d"), X[:, bass.ds(t, 1), :]).then_inc(stored, 16)
                with sp.Fori(NT - STAGES, NT) as t:
                    sp.wait_ge(used, t + STAGES + 1)
                    sp.dma_start(out[bass.ds(t, 1)].rearrange("n p d -> p n d"), X[:, bass.ds(t, 1), :]).then_inc(stored, 16)
                sp.wait_ge(stored, 16 * NT)
def flamingo_two_layers(nc, ins, out):
    with ExitStack() as ctx:
        c = Core(nc, ctx)
        a = dict(ins)
        a["out"] = out
        a["X"] = c.sb("x", [P, NT, D])
        a["XN"] = c.sb("xn", [P, NT, D])
        a["ident"] = c.sb("ident", [P, P])
        a["gates"] = c.sb("gates", [P, 4])
        a["banks"] = ctx.enter_context(nc.psum_tensor("banks", [P, 8, 512], F32))
        a["bank"] = [a["banks"][:, i, :] for i in range(8)]
        a["xt_hi"] = c.sb("xt_hi", [P, DC, T], F32R)
        a["xt_lo"] = c.sb("xt_lo", [P, DC, T], F32R)
        slots_d = nc.dram_tensor("slot_rows_d", (SLOTS + 4 * ITER, D), F32).ap()
        y_d = nc.dram_tensor("expert_rows_d", (SLOTS + 2 * ITER, D), F32).ap()
        clear = Clear(c, slots_d)
        a["carrier"] = c.sem("wait_carrier")
        with ExitStack() as ctx0:
            c0 = Core(nc, ctx0)
            w1 = Split(c0, "ffn0_gu", [P, DC, 2 * HIDDEN], chunks_of(a["w0gu"], D), I32)
            w2 = Split(c0, "ffn0_down", [P, HIDDEN // P, D], chunks_of(a["w0down"], HIDDEN), I32)
            old_sems = l0_attention(nc, a, [w1, w2])
            l0_ffn(nc, a, w1, w2, old_sems)
        with ExitStack() as ctx1:
            c1 = Core(nc, ctx1)
            VA = c1.sb("values", [P, KT, NH, VW])
            stacks = [(c1.sb(f"q_stack{i}", [P, T], F32R), c1.sb(f"k_stack{i}", [P, SK], F32R)) for i in range(2)]
            q_d, k_d = ([nc.dram_tensor(f"{n}_{part}", (D, w), F32).ap() for part in ("hi", "lo")]
                        for n, w in (("queries", T), ("keys", SK)))
            l1_projections(nc, a, VA, q_d, k_d, stacks)
            l1_attention(nc, a, VA, q_d, k_d, stacks, clear)
            l1_output(nc, a)
        R = {"IDX": c.sb("slot_of", [P, NT, TOP], U32), "IDY": c.sb("row_of", [P, NT, TOP], U32),
             "W8": c.sb("weight_of", [P, NT, TOP]), "SH": c.sb("shared_out", [P, NT, D]),
             "EXPERT_OF": c.sb("expert_of_tile", [1, 2 * P], I32), "RING_OF": c.sb("ring_place_of_tile", [1, 2 + 2 * P], I32),
             "STEPS": c.sb("step_count", [1, 1], I32),
             "WORD": c.sb("step_word", [1, P], I32), "SPAN": c.sb("step_span", [1, P], I32)}
        route_and_share(nc, a, R, slots_d, clear)
        experts(nc, a, R, slots_d, y_d, clear)
        combine(nc, a, R, y_d)


def laid_out(inputs):
    import numpy as np
    i = {n: np.asarray(v) for n, v in inputs.items()}
    ctx = i["ctx_1024"][0]
    heads = np.arange(P) // HD
    l0, l1 = "L0_xattn_", "L1_xattn_"
    return {
        "x": i["x"],
        "ctx": ctx,
        "mask": i["mask_Bx1xSxS2_bf0"].reshape(T, S2),
        "gates_d": np.stack([i["g_xattn"][0], i["g_ffn"][0], i["g_xattn"][1], i["g_ffn"][1]]),
        "w0kv": np.concatenate([np.concatenate([i[l0 + "wk_w"].T, i[l0 + "wv_w"].T], 1),
                                np.concatenate([i[l0 + "wk_b"], i[l0 + "wv_b"]])[None]], 0),
        "w0q": i[l0 + "wq_w"],
        "b0q": i[l0 + "wq_b"].reshape(DC, P).T,
        "w0o": i[l0 + "wo_w"].T,
        "b0o": i[l0 + "wo_b"],
        "ln_g": i[l0 + "ln_g"],
        "ln_b": i[l0 + "ln_b"],
        "w0gu": np.concatenate([i["L0_ffn_w_gate"].T, i["L0_ffn_w_up"].T], 1),
        "w0down": i["L0_ffn_w_down"].T,
        "w1qkv": np.concatenate([i[l1 + n].T for n in ("Wq", "Wk", "Wv")], 1),
        "b1qk": np.concatenate([i[l1 + n].reshape(DC, P).T for n in ("bq", "bk")], 1),
        "b1v": i[l1 + "bv"],
        "w1o": i[l1 + "Wo"].T,
        "b1o": i[l1 + "bo"],
        "ctx_t": np.concatenate([ctx, np.repeat(ctx[-1:], SK - S2, 0)]).T,
        "w1gate": i["L1_ffn_gate_w"].T,
        "gate_bias": i["L1_ffn_gate_bias"],
        "w1sgu": np.concatenate([i["L1_ffn_Sg"].T, i["L1_ffn_Su"].T], 1),
        "w1sdown": i["L1_ffn_Sd"].T,
        "w1gu": np.concatenate([i["L1_ffn_Wg"].transpose(0, 2, 1), i["L1_ffn_Wu"].transpose(0, 2, 1)], 2),
        "w1down": i["L1_ffn_Wd"].transpose(0, 2, 1),
        "tri_g_d": np.tril(np.ones((NG, NG), np.float32), -1).reshape(-1),
        "tri_d": np.triu(np.ones((P, P), np.float32), 1),
        "tile_numbers_d": np.arange(2 * P, dtype=np.float32).reshape(2, P).T,
        "ident_d": np.eye(P, dtype=np.float32),
        "head_mask_d": np.where(heads[:, None] == heads[None], 1 / np.sqrt(HD), 0).astype(np.float32),
    }


def kernel(**inputs):
    import numpy as np
    import concourse.bacc as bacc
    from concourse.bass_utils import run_bass_kernel_spmd
    arrays = {n: np.ascontiguousarray(v) for n, v in laid_out(inputs).items()}
    nc = bacc.Bacc("TRN2", target_bir_lowering=False, num_devices=1)
    ins = {n: nc.dram_tensor("in_" + n, v.shape, mybir.dt.from_np(v.dtype), kind="ExternalInput").ap()
           for n, v in arrays.items()}
    out = nc.dram_tensor("out", (1, T, D), F32, kind="ExternalOutput").ap()
    flamingo_two_layers(nc, ins, out)
    r = run_bass_kernel_spmd(nc, [{"in_" + n: v for n, v in arrays.items()}], core_ids=[0])
    return r.results[0]["out"]
```
